# Optimizing a Trainium2 kernel written in Bass

```python
import numpy as np
import jax
import jax.numpy as jnp

def _softmax(x, axis=-1):
    return jax.nn.softmax(x, axis=axis)

def _gelu(x):
    return jax.nn.gelu(x, approximate=True)

def _silu(x):
    return jax.nn.silu(x)

def _sigmoid(x):
    return jax.nn.sigmoid(x)

def _layernorm(x, axis=-1, eps=1e-05):
    m = jnp.mean(x, axis=axis, keepdims=True)
    v = jnp.var(x, axis=axis, keepdims=True)
    return (x - m) / jnp.sqrt(v + eps)

def _scatter_add(tgt, idx, src, axis=0):
    return tgt.at[idx].add(src)

def _segment_sum(src, seg, n):
    return jax.ops.segment_sum(src, seg, n)
kernel_name = 'mk_prb_d1_jaxref_r8_e2b032'

def setup_inputs(seed: int=0):
    np.random.seed(seed)
    _w = jnp.asarray

    def _L0_attn_setup():
        import jax, jax.numpy as jnp
        import numpy as np
        B, S, E, H, D = (4, 256, 128, 16, 64)

        def _large_negative_number(dtype):
            return jnp.asarray(-0.7 * jnp.finfo(dtype).max, dtype=dtype)
        key = jax.random.key(seed)
        k1, k2, k3 = jax.random.split(key, 3)
        x = jax.random.normal(k1, (B, S, E), dtype=jnp.float32)
        qkv_w = jax.random.normal(k2, (E, H, 3 * D), dtype=jnp.float32) * (1.0 / np.sqrt(E))
        qkv_b = jnp.zeros((H, 3 * D), dtype=jnp.float32)
        out_w = jax.random.normal(k3, (H, D, E), dtype=jnp.float32) * (1.0 / np.sqrt(H * D))
        out_b = jnp.zeros((E,), dtype=jnp.float32)
        return {'x': x, 'qkv_w': qkv_w, 'qkv_b': qkv_b, 'out_w': out_w, 'out_b': out_b}
    _L0_attn_in = _L0_attn_setup()

    def _L0_ffn_setup():
        import jax, jax.numpy as jnp
        import numpy as np
        DIM = 128

        def _reference_tuple_inner(x, W_r, W_k, W_v, mu_r, mu_k):
            B, T, C = x.shape
            x_prev = jnp.concatenate([jnp.zeros((B, 1, C), x.dtype), x[:, :-1, :]], axis=1)
            xr = mu_r * x + (1.0 - mu_r) * x_prev
            xk = mu_k * x + (1.0 - mu_k) * x_prev
            r = jax.nn.sigmoid(jnp.einsum('btc,dc->btd', xr, W_r))
            k = jnp.einsum('btc,dc->btd', xk, W_k)
            k_act = jnp.square(jax.nn.relu(k))
            out = r * jnp.einsum('btc,dc->btd', k_act, W_v)
            new_state = x[:, -1, :]
            return (out, new_state)
        key = jax.random.key(seed)
        ks = jax.random.split(key, 6)
        B, T, C = (8, 256, DIM)
        x = jax.random.normal(ks[0], (B, T, C), dtype=jnp.float32)
        s = 1.0 / np.sqrt(C)
        W_r = jax.random.uniform(ks[1], (C, C), jnp.float32, -s, s)
        W_k = jax.random.uniform(ks[2], (C, C), jnp.float32, -s, s)
        W_v = jax.random.uniform(ks[3], (C, C), jnp.float32, -s, s)
        mu_r = jax.random.uniform(ks[4], (C,), jnp.float32)
        mu_k = jax.random.uniform(ks[5], (C,), jnp.float32)
        return {'x': x, 'W_r': W_r, 'W_k': W_k, 'W_v': W_v, 'mu_r': mu_r, 'mu_k': mu_k}
    _L0_ffn_in = _L0_ffn_setup()
    _d = {'L0_attn_x': _L0_attn_in['x'], 'L0_attn_qkv_w': _L0_attn_in['qkv_w'], 'L0_attn_qkv_b': _L0_attn_in['qkv_b'], 'L0_attn_out_w': _L0_attn_in['out_w'], 'L0_attn_out_b': _L0_attn_in['out_b'], 'L0_ffn_W_r': _L0_ffn_in['W_r'], 'L0_ffn_W_k': _L0_ffn_in['W_k'], 'L0_ffn_W_v': _L0_ffn_in['W_v'], 'L0_ffn_mu_r': _L0_ffn_in['mu_r'], 'L0_ffn_mu_k': _L0_ffn_in['mu_k']}
    _x0 = _d['L0_attn_x']
    _d['L0_attn_x'] = jax.random.normal(jax.random.fold_in(jax.random.key(seed), 1), (16, 256, 128), dtype=_x0.dtype)
    del _x0
    return _d

def reference(L0_attn_x, L0_attn_qkv_w, L0_attn_qkv_b, L0_attn_out_w, L0_attn_out_b, L0_ffn_W_r, L0_ffn_W_k, L0_ffn_W_v, L0_ffn_mu_r, L0_ffn_mu_k):

    def _L0_attn_ref(x, qkv_w, qkv_b, out_w, out_b):
        import jax, jax.numpy as jnp
        import numpy as np
        B, S, E, H, D = (4, 256, 128, 16, 64)

        def _large_negative_number(dtype):
            return jnp.asarray(-0.7 * jnp.finfo(dtype).max, dtype=dtype)
        qkv = jnp.einsum('bse,ehd->bshd', x, qkv_w) + qkv_b
        q, k, v = jnp.split(qkv, 3, axis=-1)
        logits = jnp.einsum('bqhd,bkhd->bhqk', q, k)
        logits = logits / jnp.sqrt(jnp.asarray(q.shape[-1], logits.dtype))
        mask = jnp.tril(jnp.ones((q.shape[1], q.shape[1]), dtype=jnp.bool_))
        logits = jnp.where(mask, logits, _large_negative_number(logits.dtype))
        probs = jax.nn.softmax(logits, axis=-1)
        attn = jnp.einsum('bhqk,bkhd->bqhd', probs, v)
        return jnp.einsum('bqhd,hde->bqe', attn, out_w) + out_b

    def _L0_ffn_ref(x, W_r, W_k, W_v, mu_r, mu_k):
        import jax, jax.numpy as jnp
        import numpy as np
        DIM = 128

        def _reference_tuple_inner(x, W_r, W_k, W_v, mu_r, mu_k):
            B, T, C = x.shape
            x_prev = jnp.concatenate([jnp.zeros((B, 1, C), x.dtype), x[:, :-1, :]], axis=1)
            xr = mu_r * x + (1.0 - mu_r) * x_prev
            xk = mu_k * x + (1.0 - mu_k) * x_prev
            r = jax.nn.sigmoid(jnp.einsum('btc,dc->btd', xr, W_r))
            k = jnp.einsum('btc,dc->btd', xk, W_k)
            k_act = jnp.square(jax.nn.relu(k))
            out = r * jnp.einsum('btc,dc->btd', k_act, W_v)
            new_state = x[:, -1, :]
            return (out, new_state)
        return _reference_tuple_inner(x, W_r, W_k, W_v, mu_r, mu_k)[0]
    x = L0_attn_x
    xn = _layernorm(x, axis=-1)
    x = x + _L0_attn_ref(xn, L0_attn_qkv_w, L0_attn_qkv_b, L0_attn_out_w, L0_attn_out_b) + _L0_ffn_ref(xn, L0_ffn_W_r, L0_ffn_W_k, L0_ffn_W_v, L0_ffn_mu_r, L0_ffn_mu_k)
    return x

_drawn_inputs = setup_inputs


def setup_inputs(seed=0):
    import zlib

    import numpy as np

    out = dict(_drawn_inputs(seed))
    spreads = {'L0_attn_qkv_b': (0.0, 0.1), 'L0_attn_out_b': (0.0, 0.1)}
    factors = {'L0_ffn_W_r': 3.264, 'L0_ffn_mu_r': 6.42}
    for name, (base, spread) in spreads.items():
        noise = np.random.default_rng([zlib.crc32(name.encode()), seed]).standard_normal(out[name].shape)
        drawn = base * np.exp(spread * noise) if base else spread * noise
        out[name] = jnp.asarray(drawn.astype(out[name].dtype))
    for name, factor in factors.items():
        out[name] = (out[name] * factor).astype(out[name].dtype)
    return out
```

```python
from contextlib import ExitStack

import concourse.bass as bass
from concourse import mybir

ALU = mybir.AluOpType
ACT = mybir.ActivationFunctionType
F32 = mybir.dt.float32
F32R = mybir.dt.float32r

P = 128
BATCHES, TOKENS, E = 16, 256, 128
HEADS, D = 16, 64
PAIRS = HEADS // 2
QB = TOKENS // P
CAUSAL = P + TOKENS
HALF = HEADS * D // 2
EPS = 1e-5
MASKED = -0.7 * 3.4028234663852886e38
LOWEST = -3.4e38

SLOTS = HEADS
TURN = 6
TURN_LAG, PV_LAG, OUT_LAG = 2, 3, 4

SIDE = {0: ("v", 0, 1), 1: ("qk", 4), 2: ("qk", 5), 3: ("mix_rk",), 4: ("qk", 6), 5: ("v", 1, 0),
        6: ("v", 1, 1), 7: ("qk", 7), 8: ("mix_v",), 9: ("xT",), 11: ("qk", 0), 12: ("qk", 1),
        13: ("qk", 2), 14: ("qk", 3), 15: ("v", 0, 0)}
KINDS = {s[0] for s in SIDE.values()}
FIRST = 9
START = 6 - SLOTS


class Slot:

    def __init__(self, turn, c):
        self.turn, self.c = turn, c
        self.t = c % SLOTS

    def back(self, n):
        return Slot(self.turn, self.c - n)

    def number(self):
        return self.turn * SLOTS + self.c if isinstance(self.turn, int) else None

    def batch(self, ahead=0):
        n = self.number()
        return n is None or 0 <= n // SLOTS + ahead < BATCHES

    def side_exists(self):
        return self.t in SIDE and self.batch(self.t >= FIRST)

    def count(self, per_window, so_far):
        return self.turn * per_window + (self.c // SLOTS) * per_window + so_far

    def heads(self):
        return self.count(SLOTS, self.t + 1)

    def pairs(self):
        return self.count(PAIRS, self.t // 2 + 1)

    def side(self, kind):
        slots = [s for s, what in SIDE.items() if what[0] == kind]
        return self.count(len(slots), sum(s >= FIRST for s in slots) + sum(s <= self.t for s in slots))

    def last_in_bank(self):
        return next(s for s in (self.back(n) for n in range(2, SLOTS, 2)) if s.t in SIDE)


def build(nc, x, xT, qkv_w, qkv_b, out_w, out_b, w_r, w_k, w_v, mu_r, mu_k, outT):
    with ExitStack() as ctx:
        def sb(name, shape, dt=F32):
            return ctx.enter_context(nc.sbuf_tensor(name, shape, dt))

        def bank(name):
            return ctx.enter_context(nc.psum_tensor(name, [P, 512], F32))

        def sem(name):
            return ctx.enter_context(nc.semaphore(name))

        wqkv = sb("wqkv", [E, HEADS, 3 * D])
        wq = [sb("wq_hi", [E, HEADS, D], F32R), sb("wq_lo", [E, HEADS, D], F32R)]
        wk = [sb("wk_hi", [E, HEADS, D], F32R), sb("wk_lo", [E, HEADS, D], F32R)]
        wv = [sb("wv_hi", [E, HEADS, D], F32R), sb("wv_lo", [E, HEADS, D], F32R)]
        bias = sb("bias", [P, 3, PAIRS])
        wo = sb("wo", [P, PAIRS, E])
        bo = sb("bo", [E, 1])
        bo_all = sb("bo_all", [E, 1])
        wr_sb, wk_sb, wv_sb = sb("mix_wr", [E, E]), sb("mix_wk", [E, E]), sb("mix_wv", [E, E])
        mu = sb("mu", [E, 2])
        mu_rest = sb("mu_rest", [E, 2])
        ident = sb("ident", [P, P])
        mask = sb("mask", [P, CAUSAL])
        rsqrt_exp = sb("rsqrt_exp", [P, QB])
        eps = sb("eps", [P, QB])
        neg_scale = sb("neg_scale", [P, QB])
        clear = sb("clear", [P, 5])

        x_in = sb("x_in", [P, QB, E])
        stats = sb("stats", [P, QB, 6])
        mean_var = sb("mean_var", [P, QB, 2])
        var_eps = sb("var_eps", [P, QB])
        rstd = sb("rstd", [P, QB])
        xn = sb("xn", [P, QB, E])
        xnT = sb("xnT", [E, 1 + TOKENS])
        xnT_hi, xnT_lo = sb("xnT_hi", [E, TOKENS], F32R), sb("xnT_lo", [E, TOKENS], F32R)
        qT, kT = sb("qT", [P, PAIRS, TOKENS]), sb("kT", [P, PAIRS, TOKENS])
        v = sb("v", [P, QB, HEADS * D])
        x_res = sb("x_res", [E, TOKENS])
        x_rest = sb("x_rest", [E, 2, TOKENS])
        x_mix = sb("x_mix", [E, 2, TOKENS])
        r_tanh = sb("r_tanh", [E, TOKENS])
        k_relu = sb("k_relu", [E, TOKENS])
        k_act = sb("k_act", [E, TOKENS])
        gated = sb("gated", [E, TOKENS])
        rest = sb("rest", [E, TOKENS])
        y = sb("y", [E, TOKENS])

        scores = sb("scores", [P, 2, CAUSAL])
        top = sb("top", [P, 4, QB])
        neg_top = sb("neg_top", [P, 4, QB])
        probs = sb("probs", [P, 4, CAUSAL])
        total = sb("total", [P, 4, QB])
        inv_total = sb("inv_total", [P, 4, QB])
        probsT = sb("probsT", [P, 4, CAUSAL])
        attnT = sb("attnT", [P, 2, TOKENS])

        ps_scores = [bank("ps_scores0"), bank("ps_scores1")]
        ps_turn = [bank("ps_turn0"), bank("ps_turn1")]
        ps_attn = bank("ps_attn")
        ps_out = bank("ps_out")
        ps_side = [bank("ps_side0"), bank("ps_side1")]

        weights_in = sem("weights_in")
        x_in_loaded = sem("x_in_loaded")
        x_res_loaded = sem("x_res_loaded")
        y_free = sem("y_free")
        mask_parts = sem("mask_parts")
        consts_ready = sem("consts_ready")
        hi_ready = sem("hi_ready")
        weights_split = sem("weights_split")
        bias_product = sem("bias_product")
        bias_ready = sem("bias_ready")
        stats_done = sem("stats_done")
        mean_done = sem("mean_done")
        var_done = sem("var_done")
        rstd_done = sem("rstd_done")
        xn_done = sem("xn_done")
        xnT_done = sem("xnT_done")
        xnT_hi_done = sem("xnT_hi_done")
        xnT_split = sem("xnT_split")
        side_done = {k: sem(f"side_{k}_done") for k in sorted(KINDS)}
        qk_ready = sem("qk_ready")
        v_ready = sem("v_ready")
        rest_done = sem("rest_done")
        mix_done = sem("mix_done")
        relu_done = sem("relu_done")
        k_act_done = sem("k_act_done")
        gated_done = sem("gated_done")
        residue_done = sem("residue_done")
        scores_done = sem("scores_done")
        masked_done = sem("masked_done")
        neg_done = sem("neg_done")
        exp_done = sem("exp_done")
        inv_done = sem("inv_done")
        norm_done = sem("norm_done")
        turned = sem("turned")
        probsT_even = sem("probsT_even")
        probsT_odd = sem("probsT_odd")
        pv_done = sem("pv_done")
        attnT_done = sem("attnT_done")
        out_done = sem("out_done")
        y_done = sem("y_done")

        side_read = {"xT": xnT_done, "qk": qk_ready, "v": v_ready, "mix_rk": relu_done, "mix_v": gated_done}

        block = ctx.enter_context(nc.Block())
        WEIGHT_LOADS, CONSTS = 9, 6
        BLOCK_COLS = [slice(0, P), slice(P, CAUSAL)]

        def wait(eng, signal, n):
            if not isinstance(n, int) or n > 0:
                eng.wait_ge(signal, n)

        def run(eng, slot_work, last=SLOTS + OUT_LAG):
            for c in range(START, TURN):
                slot_work(Slot(0, c))
            with eng.Fori(0, BATCHES - 1) as turn:
                for c in range(TURN, TURN + SLOTS):
                    slot_work(Slot(turn, c))
            for c in range(TURN, last + 1):
                slot_work(Slot(BATCHES - 1, c))

        def rows(first):
            return x[first, :].rearrange("(b p) e -> p b e", p=P)

        @block.sync
        def _(sync):
            sync.dma_start(x_in[:], rows(slice(0, TOKENS))).then_inc(x_in_loaded, 16)
            sync.dma_start(wqkv[:], qkv_w).then_inc(weights_in, 16)
            sync.dma_start(bias[:], qkv_b).then_inc(weights_in, 16)
            sync.dma_start(wr_sb[:], w_r).then_inc(weights_in, 16)
            sync.dma_start(wk_sb[:], w_k).then_inc(weights_in, 16)
            sync.dma_start(wv_sb[:], w_v).then_inc(weights_in, 16)
            sync.dma_start(mu[:, 0:1], mu_r).then_inc(weights_in, 16)
            sync.dma_start(mu[:, 1:2], mu_k).then_inc(weights_in, 16)
            sync.dma_start(bo[:], out_b).then_inc(weights_in, 16)
            sync.dma_start(wo[:], out_w.rearrange("(c p) e -> p c e", p=P)).then_inc(weights_in, 16)
            sync.dma_start(x_res[:], xT[:, 0:TOKENS]).then_inc(x_res_loaded, 16)
            sync.wait_ge(xn_done, 1)
            sync.dma_start(x_in[:], rows(slice(TOKENS, 2 * TOKENS))).then_inc(x_in_loaded, 16)

            def load_x(done, tokens):
                sync.wait_ge(xn_done, done)
                sync.dma_start(x_in[:], rows(tokens)).then_inc(x_in_loaded, 16)

            def load_residual(done, tokens):
                sync.wait_ge(residue_done, done)
                sync.dma_start(x_res[:], xT[:, tokens]).then_inc(x_res_loaded, 16)

            def store(done, tokens):
                sync.wait_ge(y_done, done)
                sync.dma_start(outT[:, tokens], y[:]).then_inc(y_free, 16)

            with sync.Fori(2, BATCHES) as b:
                load_x(b, bass.ds(b * TOKENS, TOKENS))
                load_residual(b - 1, bass.ds(b * TOKENS - TOKENS, TOKENS))
                store(b - 1, bass.ds(b * TOKENS - 2 * TOKENS, TOKENS))
            end = BATCHES * TOKENS
            load_residual(BATCHES - 1, slice(end - TOKENS, end))
            store(BATCHES - 1, slice(end - 2 * TOKENS, end - TOKENS))
            store(BATCHES, slice(end - TOKENS, end))
            sync.wait_ge(y_free, 16 * (BATCHES + 1))

        @block.gpsimd
        def _(pool):
            pool.memset(ident[:], 0.0).then_inc(mask_parts, 1)
            pool.memset(mask[:], 0.0).then_inc(mask_parts, 1)
            pool.memset(xnT[:, 0:1], 0.0).then_inc(mask_parts, 1)
            pool.memset(y[:], 0.0).then_inc(y_free, 16)
            pool.memset(rsqrt_exp[:], -0.5).then_inc(consts_ready, 1)
            pool.memset(eps[:], EPS).then_inc(consts_ready, 1)
            pool.memset(neg_scale[:], -D ** -0.5).then_inc(consts_ready, 1)
            pool.wait_ge(mask_parts, 3)
            pool.affine_select(out=ident[:], in_=ident[:], compare_op=ALU.not_equal, fill=1.0, base=0,
                               pattern=[[-1, P]], channel_multiplier=1).then_inc(consts_ready, 1)
            for diagonal in (slice(0, P), slice(CAUSAL - P, CAUSAL)):
                pool.affine_select(out=mask[:, diagonal], in_=mask[:, diagonal], compare_op=ALU.is_ge,
                                   fill=MASKED, base=0, pattern=[[-1, P]],
                                   channel_multiplier=1).then_inc(consts_ready, 1)
            pool.wait_ge(consts_ready, CONSTS)

            def slot_work(s):
                if s.batch():
                    ring = s.t % 4
                    wait(pool, masked_done, s.heads())
                    wait(pool, exp_done, s.back(4).heads())
                    pool.tensor_tensor(neg_top[:, ring, :], top[:, ring, :], neg_scale[:],
                                       ALU.mult).then_inc(neg_done, 1)
                if s.t == 6 and s.batch(1):
                    wait(pool, mean_done, s.count(1, 2))
                    pool.tensor_tensor(var_eps[:], mean_var[:, :, 1], eps[:], ALU.add).then_inc(var_done, 1)
                    wait(pool, var_done, s.count(1, 2))
                    wait(pool, xn_done, s.count(1, 1))
                    pool.tensor_tensor(rstd[:], var_eps[:], rsqrt_exp[:], ALU.pow).then_inc(rstd_done, 1)
                if s.t == 4 and s.batch():
                    wait(pool, relu_done, s.count(1, 1))
                    pool.tensor_tensor(k_act[:], k_relu[:], k_relu[:], ALU.mult).then_inc(k_act_done, 1)

            run(pool, slot_work)

        @block.tensor
        def _(pe):
            pe.wait_ge(consts_ready, CONSTS)
            pe.wait_ge(weights_in, 16 * WEIGHT_LOADS)
            for j in range(PAIRS):
                mm = pe.matmul(ps_out[:, 0:1], wo[:, j, :], bias[:, 2, j:j + 1],
                               start=(j == 0), stop=(j == PAIRS - 1))
            mm.then_inc(bias_product, 1)

            def split_product(out, weights, acts):
                parts = ((0, 0), (0, 1), (1, 0))
                for n, (a, b) in enumerate(parts):
                    mm = pe.matmul(out, weights[a], acts[b], start=(n == 0), stop=(n == len(parts) - 1))
                return mm

            def side_work(s):
                kind, *what = SIDE[s.t]
                out = ps_side[s.t % 2]
                ahead = s.t >= FIRST
                last = s.last_in_bank()
                if last.side_exists():
                    last_kind = SIDE[last.t][0]
                    wait(pe, side_read[last_kind], last.side(last_kind))
                if kind == "xT":
                    wait(pe, xn_done, s.count(1, 2))
                    for b in range(QB):
                        mm = pe.transpose(out[:, b * P:(b + 1) * P], xn[:, b, :], ident[:])
                elif kind == "qk":
                    if what[0] == 0:
                        pe.wait_ge(weights_split, 3)
                    wait(pe, xnT_split, s.count(1, 1 + ahead))
                    pair = slice(2 * what[0], 2 * what[0] + 2)
                    acts = (xnT_hi[:], xnT_lo[:])
                    split_product(out[:, 0:TOKENS], [w[:, pair, :] for w in wq], acts)
                    mm = split_product(out[:, TOKENS:2 * TOKENS], [w[:, pair, :] for w in wk], acts)
                elif kind == "v":
                    half, b = what
                    wait(pe, xnT_split, s.count(1, 1 + ahead))
                    tokens = slice(b * P, (b + 1) * P)
                    heads = slice(half * PAIRS, (half + 1) * PAIRS)
                    mm = split_product(out[:], (xnT_hi[:, tokens], xnT_lo[:, tokens]),
                                       [w[:, heads, :] for w in wv])
                elif kind == "mix_rk":
                    wait(pe, mix_done, s.count(1, 1))
                    pe.matmul(out[:, 0:TOKENS], wr_sb[:], x_mix[:, 0, :], start=True, stop=True)
                    mm = pe.matmul(out[:, TOKENS:2 * TOKENS], wk_sb[:], x_mix[:, 1, :], start=True, stop=True)
                elif kind == "mix_v":
                    wait(pe, k_act_done, s.count(1, 1))
                    mm = pe.matmul(out[:, 0:TOKENS], wv_sb[:], k_act[:], start=True, stop=True)
                mm.then_inc(side_done[kind], 1)

            def slot_work(s):
                if s.batch():
                    pair, at = s.t // 2, slice(D * (s.t % 2), D * (s.t % 2) + D)
                    wait(pe, qk_ready, s.pairs())
                    wait(pe, masked_done, s.back(2).heads())
                    for b, cols in enumerate(BLOCK_COLS):
                        mm = pe.matmul(ps_scores[s.t % 2][:, cols], qT[at, pair, b * P:(b + 1) * P],
                                       kT[at, pair, 0:(b + 1) * P], start=True, stop=True)
                    mm.then_inc(scores_done, 1)
                if s.side_exists():
                    side_work(s)
                u = s.back(TURN_LAG)
                if u.batch():
                    wait(pe, norm_done, u.heads())
                    wait(pe, (probsT_even, probsT_odd)[u.t % 2], u.back(2).pairs())
                    for k in range(CAUSAL // P):
                        cols = slice(k * P, (k + 1) * P)
                        mm = pe.transpose(ps_turn[u.t % 2][:, cols], probs[:, u.t % 4, cols], ident[:])
                    mm.then_inc(turned, 1)
                u = s.back(PV_LAG)
                if u.batch() and u.t % 2:
                    wait(pe, probsT_even, u.pairs())
                    wait(pe, probsT_odd, u.pairs())
                    wait(pe, v_ready, u.count(4, 2 if u.t < PAIRS else 4))
                    wait(pe, attnT_done, u.back(2).pairs())
                    for k, (queries, cols) in enumerate(((slice(0, TOKENS), slice(0, TOKENS)),
                                                         (slice(P, TOKENS), slice(TOKENS, CAUSAL)))):
                        for n in range(2):
                            h = u.t - 1 + n
                            mm = pe.matmul(ps_attn[D * n:D * n + D, queries], v[:, k, h * D:(h + 1) * D],
                                           probsT[:, h % 4, cols], start=(k == 0), stop=(k == QB - 1))
                    mm.then_inc(pv_done, 1)
                u = s.back(OUT_LAG)
                if u.batch() and u.t % 2:
                    j = u.t // 2
                    wait(pe, attnT_done, u.pairs())
                    if j == 0:
                        pe.wait_ge(bias_ready, 1)
                        wait(pe, y_done, u.count(1, 0))
                    pe.matmul(ps_out[:, 0:TOKENS], wo[:, j, :], attnT[:, j % 2, :],
                              start=(j == 0), stop=(j == PAIRS - 1)).then_inc(out_done, 1)

            run(pe, slot_work)

        @block.scalar
        def _(act):
            act.wait_ge(weights_in, 16 * WEIGHT_LOADS)
            for n, w in enumerate((wq, wk, wv)):
                act.copy(w[0][:], wqkv[:, :, n * D:(n + 1) * D]).then_inc(hi_ready, 1)

            def side_work(s):
                kind, *what = SIDE[s.t]
                out = ps_side[s.t % 2]
                if kind == "qk":
                    p = what[0]
                    wait(act, side_done["qk"], s.side("qk"))
                    act.activation(qT[:, p, :], out[:, 0:TOKENS], ACT.Identity, bias=bias[:, 0, p:p + 1])
                    mm = act.activation(kT[:, p, :], out[:, TOKENS:2 * TOKENS], ACT.Identity,
                                        bias=bias[:, 1, p:p + 1])
                    mm.then_inc(qk_ready, 1)
                elif kind == "xT":
                    wait(act, side_done["xT"], s.side("xT"))
                    wait(act, mix_done, s.count(1, 1))
                    wait(act, xnT_split, s.count(1, 1))
                    if s.number() is not None and s.number() < 0:
                        act.wait_ge(mask_parts, 3)
                    act.copy(xnT[:, 1:], out[:, 0:TOKENS]).then_inc(xnT_done, 1)
                elif kind == "mix_rk":
                    wait(act, side_done["mix_rk"], s.side("mix_rk"))
                    wait(act, gated_done, s.count(1, 0))
                    act.activation(r_tanh[:], out[:, 0:TOKENS], ACT.Tanh, scale=0.5)
                    act.activation(k_relu[:], out[:, TOKENS:2 * TOKENS],
                                   ACT.Relu).then_inc(relu_done, 1)

            def slot_work(s):
                u = s.back(OUT_LAG)
                if u.batch() and u.t % 2:
                    wait(act, pv_done, u.pairs())
                    act.copy(attnT[:, u.t // 2 % 2, :], ps_attn[:, 0:TOKENS]).then_inc(attnT_done, 1)
                if s.side_exists():
                    side_work(s)
                u = s.back(TURN_LAG)
                if u.batch() and u.t % 2:
                    wait(act, turned, u.heads())
                    wait(act, pv_done, u.back(4).pairs())
                    act.copy(probsT[:, u.t % 4, :], ps_turn[1][:, 0:CAUSAL]).then_inc(probsT_odd, 1)
                if s.batch():
                    ring = s.t % 4
                    wait(act, neg_done, s.heads())
                    wait(act, turned, s.back(4).heads())
                    for b, cols in enumerate(BLOCK_COLS):
                        last = act.activation(probs[:, ring, cols], scores[:, s.t % 2, cols], ACT.Exp,
                                              bias=neg_top[:, ring, b:b + 1], scale=D ** -0.5,
                                              accum_out=total[:, ring, b:b + 1])
                    last.then_inc(exp_done, 1)

            run(act, slot_work)

        @block.vector
        def _(dve):
            for n, w in enumerate((wq, wk, wv)):
                dve.wait_ge(hi_ready, n + 1)
                dve.tensor_tensor(w[1][:], wqkv[:, :, n * D:(n + 1) * D], w[0][:].bitcast(F32),
                                  ALU.subtract).then_inc(weights_split, 1)
            dve.tensor_scalar(mu_rest[:], mu[:], -1.0, 1.0, ALU.mult, ALU.add).then_inc(bias_ready, 1)
            dve.wait_ge(bias_product, 1)
            dve.tensor_tensor(bo_all[:], ps_out[:, 0:1], bo[:], ALU.add).then_inc(bias_ready, 1)
            dve.wait_ge(consts_ready, CONSTS)
            dve.wait_ge(bias_ready, 2)

            def side_work(s):
                if s.t in SIDE and SIDE[s.t][0] == "v" and s.side_exists():
                    half, b = SIDE[s.t][1:]
                    wait(dve, side_done["v"], s.side("v"))
                    dve.tensor_copy(v[:, b, half * HALF:(half + 1) * HALF],
                                    ps_side[s.t % 2][:]).then_inc(v_ready, 1)
                if s.t == 4 and s.batch(-1):
                    wait(dve, out_done, s.count(PAIRS, 0))
                    wait(dve, residue_done, s.count(1, 0))
                    wait(dve, y_free, s.count(16, 0))
                    dve.scalar_tensor_tensor(out=y[:], in0=ps_out[:, 0:TOKENS], scalar=bo_all[:, 0:1],
                                             in1=rest[:], op0=ALU.add, op1=ALU.add).then_inc(y_done, 1)
                if s.t == 6 and s.batch(1):
                    wait(dve, x_in_loaded, s.count(16, 32))
                    for b in range(QB):
                        last = dve.bn_stats(stats[:, b, :], x_in[:, b, :])
                    last.then_inc(stats_done, 1)
                    wait(dve, stats_done, s.count(1, 2))
                    wait(dve, rstd_done, s.count(1, 1))
                    dve.memset(clear[:, 4:5], 0.0)
                    for b in range(QB):
                        last = dve.bn_aggr(mean_var[:, b, :], stats[:, b, :])
                    last.then_inc(mean_done, 1)
                if s.t == 7 and s.batch(1):
                    wait(dve, rstd_done, s.count(1, 2))
                    wait(dve, side_done["xT"], s.count(1, 1))
                    for b in range(QB):
                        last = dve.tensor_scalar(xn[:, b, :], x_in[:, b, :], mean_var[:, b, 0:1],
                                                 rstd[:, b:b + 1], ALU.subtract, ALU.mult)
                    last.then_inc(xn_done, 1)
                if s.t == 9 and s.batch():
                    wait(dve, side_done["mix_v"], s.count(1, 1))
                    dve.scalar_tensor_tensor(out=gated[:], in0=r_tanh[:], scalar=1.0, in1=ps_side[0][:, 0:TOKENS],
                                             op0=ALU.add, op1=ALU.mult).then_inc(gated_done, 1)
                    wait(dve, gated_done, s.count(1, 1))
                    wait(dve, x_res_loaded, s.count(16, 16))
                    dve.scalar_tensor_tensor(out=rest[:], in0=gated[:], scalar=0.5, in1=x_res[:],
                                             op0=ALU.mult, op1=ALU.add).then_inc(residue_done, 1)
                if s.t == 10 and s.batch(1):
                    wait(dve, xnT_done, s.count(1, 2))
                    wait(dve, side_done["qk"], s.side("qk"))
                    dve.tensor_copy(xnT_hi[:], xnT[:, 1:]).then_inc(xnT_hi_done, 1)
                    wait(dve, xnT_hi_done, s.count(1, 2))
                    dve.tensor_tensor(xnT_lo[:], xnT[:, 1:], xnT_hi[:].bitcast(F32),
                                      ALU.subtract).then_inc(xnT_split, 1)
                if s.t == 11 and s.batch(1):
                    wait(dve, mix_done, s.count(1, 1))
                    for n in range(2):
                        last = dve.tensor_scalar(x_rest[:, n, :], xnT[:, 0:TOKENS], mu_rest[:, n:n + 1], None,
                                                 ALU.mult)
                    last.then_inc(rest_done, 1)
                if s.t == 12 and s.batch(1):
                    wait(dve, rest_done, s.count(1, 2))
                    wait(dve, side_done["mix_rk"], s.count(1, 1))
                    for n in range(2):
                        last = dve.scalar_tensor_tensor(out=x_mix[:, n, :], in0=xnT[:, 1:], scalar=mu[:, n:n + 1],
                                                        in1=x_rest[:, n, :], op0=ALU.mult, op1=ALU.add)
                    last.then_inc(mix_done, 1)

            def slot_work(s):
                if s.batch():
                    wait(dve, scores_done, s.heads())
                    wait(dve, exp_done, s.back(2).heads())
                    wait(dve, neg_done, s.back(4).heads())
                    dve.memset(clear[:, s.t % 4:s.t % 4 + 1], 0.0)
                    for b, cols in enumerate(BLOCK_COLS):
                        last = dve.tensor_tensor_reduce(scores[:, s.t % 2, cols], ps_scores[s.t % 2][:, cols],
                                                        mask[:, cols], 1.0, LOWEST, ALU.add, ALU.max,
                                                        top[:, s.t % 4, b:b + 1])
                    last.then_inc(masked_done, 1)
                n = s.back(1)
                if n.batch():
                    wait(dve, exp_done, n.heads())
                    dve.reciprocal(inv_total[:, n.t % 4, :], total[:, n.t % 4, :]).then_inc(inv_done, 1)
                u = s.back(TURN_LAG)
                if u.batch() and u.t % 2 == 0:
                    wait(dve, turned, u.heads())
                    wait(dve, pv_done, u.back(4).pairs())
                    dve.tensor_copy(probsT[:, u.t % 4, :], ps_turn[0][:, 0:CAUSAL]).then_inc(probsT_even, 1)
                if n.batch():
                    wait(dve, inv_done, n.heads())
                    for b, cols in enumerate(BLOCK_COLS):
                        block_probs = probs[:, n.t % 4, cols]
                        last = dve.tensor_scalar(block_probs, block_probs, inv_total[:, n.t % 4, b:b + 1], None,
                                                 ALU.mult)
                    last.then_inc(norm_done, 1)
                side_work(s)

            run(dve, slot_work)


def kernel(L0_attn_x, L0_attn_qkv_w, L0_attn_qkv_b, L0_attn_out_w, L0_attn_out_b,
           L0_ffn_W_r, L0_ffn_W_k, L0_ffn_W_v, L0_ffn_mu_r, L0_ffn_mu_k):
    import numpy as np
    from concourse import bacc
    from concourse.bass_utils import run_bass_kernel_spmd

    flat = np.asarray(L0_attn_x).reshape(BATCHES * TOKENS, E)
    by_pair = np.asarray(L0_attn_qkv_b).reshape(PAIRS, 2, 3, D).transpose(1, 3, 2, 0).reshape(P, 3, PAIRS)
    arrays = {
        "x": flat, "xT": flat.T, "qkv_w": L0_attn_qkv_w, "qkv_b": by_pair,
        "out_w": np.asarray(L0_attn_out_w).reshape(HEADS * D, E), "out_b": np.asarray(L0_attn_out_b).reshape(E, 1),
        "w_r": np.asarray(L0_ffn_W_r).T, "w_k": np.asarray(L0_ffn_W_k).T, "w_v": np.asarray(L0_ffn_W_v).T,
        "mu_r": np.asarray(L0_ffn_mu_r).reshape(E, 1), "mu_k": np.asarray(L0_ffn_mu_k).reshape(E, 1),
    }
    arrays = {name: np.ascontiguousarray(a) for name, a in arrays.items()}
    nc = bacc.Bacc("TRN2", target_bir_lowering=False, num_devices=1)
    args = [nc.dram_tensor(name, a.shape, F32, kind="ExternalInput").ap() for name, a in arrays.items()]
    outT = nc.dram_tensor("outT", (E, BATCHES * TOKENS), F32, kind="ExternalOutput").ap()
    build(nc, *args, outT)
    r = run_bass_kernel_spmd(nc, [arrays], core_ids=[0])
    return np.ascontiguousarray(r.results[0]["outT"].T).reshape(BATCHES, TOKENS, E)
```

```python
from contextlib import ExitStack

import concourse.bass as bass
from concourse import mybir

ALU = mybir.AluOpType
ACT = mybir.ActivationFunctionType
F32 = mybir.dt.float32
F32R = mybir.dt.float32r

P = 128
BATCHES, TOKENS, E = 16, 256, 128
HEADS, D = 16, 64
PAIRS = HEADS // 2
QB = TOKENS // P
SPLIT = P + TOKENS
CAUSAL = P + TOKENS
HALF = HEADS * D // 2
EPS = 1e-5
MASKED = -0.7 * 3.4028234663852886e38
HIGHEST = 3.4e38

SLOTS = HEADS
TURN = 6
TURN_LAG, PV_LAG, OUT_LAG = 2, 3, 4

SIDE = {0: ("v", 0, 1), 1: ("qk", 4), 2: ("qk", 5), 3: ("mix_rk",), 4: ("qk", 6), 5: ("mix_v",),
        6: ("qk", 7), 7: ("v", 1, 0), 8: ("v", 1, 1), 9: ("xT",), 11: ("qk", 0), 12: ("qk", 1),
        13: ("qk", 2), 14: ("qk", 3), 15: ("v", 0, 0)}
KINDS = {s[0] for s in SIDE.values()}
FIRST = 9
START = 6 - SLOTS

CHUNKS = (slice(0, 4), slice(4, 8), slice(8, 16))
HI_AT = (-10, -9, -6)
LO_AT = (-9, -7, -4)


def chunk_of(head):
    return next(n for n, heads in enumerate(CHUNKS) if head < heads.stop)


class Slot:

    def __init__(self, turn, c):
        self.turn, self.c = turn, c
        self.t = c % SLOTS

    def back(self, n):
        return Slot(self.turn, self.c - n)

    def number(self):
        return self.turn * SLOTS + self.c if isinstance(self.turn, int) else None

    def batch(self, ahead=0):
        n = self.number()
        return n is None or 0 <= n // SLOTS + ahead < BATCHES

    def side_exists(self):
        return self.t in SIDE and self.batch(self.t >= FIRST)

    def count(self, per_window, so_far):
        return self.turn * per_window + (self.c // SLOTS) * per_window + so_far

    def heads(self):
        return self.count(SLOTS, self.t + 1)

    def pairs(self):
        return self.count(PAIRS, self.t // 2 + 1)

    def side(self, kind):
        slots = [s for s, what in SIDE.items() if what[0] == kind]
        return self.count(len(slots), sum(s >= FIRST for s in slots) + sum(s <= self.t for s in slots))

    def last_in_bank(self):
        return next(s for s in (self.back(n) for n in range(2, SLOTS, 2)) if s.t in SIDE)


def build(nc, x, xT, qkv_w, qkv_b, out_w, out_b, w_r, w_k, w_v, mu_r, mu_k, outT):
    with ExitStack() as ctx:
        def sb(name, shape, dt=F32):
            return ctx.enter_context(nc.sbuf_tensor(name, shape, dt))

        def bank(name):
            return ctx.enter_context(nc.psum_tensor(name, [P, 512], F32))

        def sem(name):
            return ctx.enter_context(nc.semaphore(name))

        wqkv = sb("wqkv", [E, HEADS, 3 * D])
        wq = [sb("wq_hi", [E, HEADS, D], F32R), sb("wq_lo", [E, HEADS, D], F32R)]
        wk = [sb("wk_hi", [E, HEADS, D], F32R), sb("wk_lo", [E, HEADS, D], F32R)]
        wv = [sb("wv_hi", [E, HEADS, D], F32R), sb("wv_lo", [E, HEADS, D], F32R)]
        bias = sb("bias", [P, 3, PAIRS])
        wo = sb("wo", [P, PAIRS, E])
        bo = sb("bo", [E, 1])
        wr_sb, wk_sb, wv_sb = sb("mix_wr", [E, E]), sb("mix_wk", [E, E]), sb("mix_wv", [E, E])
        mu = sb("mu", [E, 2])
        ident = sb("ident", [P, P])
        mask = sb("mask", [P, CAUSAL])
        rsqrt_exp = sb("rsqrt_exp", [P, QB])
        eps = sb("eps", [P, QB])
        clear = sb("clear", [P, 5])

        x_in = sb("x_in", [P, QB, E])
        stats = sb("stats", [P, QB, 6])
        mean_var = sb("mean_var", [P, QB, 2])
        var_eps = sb("var_eps", [P, QB])
        rstd = sb("rstd", [P, QB])
        xn = sb("xn", [P, QB, E])
        xnT = sb("xnT", [E, 1 + TOKENS])
        xnT_hi, xnT_lo = sb("xnT_hi", [E, TOKENS], F32R), sb("xnT_lo", [E, TOKENS], F32R)
        qk = sb("qk", [P, PAIRS, 2 * TOKENS])
        qk_hi, qk_lo = sb("qk_hi", [P, PAIRS, SPLIT], F32R), sb("qk_lo", [P, PAIRS, SPLIT], F32R)
        v = sb("v", [P, QB, HEADS * D])
        x_res = sb("x_res", [E, TOKENS])
        x_step = sb("x_step", [E, TOKENS])
        x_mix = sb("x_mix", [E, 2, TOKENS])
        r_tanh = sb("r_tanh", [E, TOKENS])
        k_relu = sb("k_relu", [E, TOKENS])
        k_act = sb("k_act", [E, TOKENS])
        gated = sb("gated", [E, TOKENS])
        rest = sb("rest", [E, TOKENS])
        y = sb("y", [E, TOKENS])

        scores = sb("scores", [P, 2, CAUSAL])
        neg_top = sb("neg_top", [P, 4, QB])
        probs = sb("probs", [P, 4, CAUSAL])
        total = sb("total", [P, 4, QB])
        inv_total = sb("inv_total", [P, 4, QB])
        probsT = sb("probsT", [P, 4, CAUSAL])
        attnT = sb("attnT", [P, 2, TOKENS])

        ps_scores = [bank("ps_scores0"), bank("ps_scores1")]
        ps_turn = [bank("ps_turn0"), bank("ps_turn1")]
        ps_attn = bank("ps_attn")
        ps_out = bank("ps_out")
        ps_side = [bank("ps_side0"), bank("ps_side1")]

        qkv_w_in = [sem(f"qkv_w_in{n}") for n in range(len(CHUNKS))]
        small_in = sem("small_in")
        weights_in = sem("weights_in")
        x_in_loaded = sem("x_in_loaded")
        x_res_loaded = sem("x_res_loaded")
        y_free = sem("y_free")
        mask_parts = sem("mask_parts")
        consts_ready = sem("consts_ready")
        hi_ready = sem("hi_ready")
        weights_split = sem("weights_split")
        stats_done = sem("stats_done")
        mean_done = sem("mean_done")
        var_done = sem("var_done")
        rstd_done = sem("rstd_done")
        xn_done = sem("xn_done")
        xnT_done = sem("xnT_done")
        xnT_hi_done = sem("xnT_hi_done")
        xnT_split = sem("xnT_split")
        side_done = {k: sem(f"side_{k}_done") for k in sorted(KINDS)}
        qk_ready = sem("qk_ready")
        qk_hi_ready = sem("qk_hi_ready")
        qk_lo_ready = sem("qk_lo_ready")
        v_ready = sem("v_ready")
        step_done = sem("step_done")
        mix_done = sem("mix_done")
        relu_done = sem("relu_done")
        k_act_done = sem("k_act_done")
        gated_done = sem("gated_done")
        residue_done = sem("residue_done")
        scores_done = sem("scores_done")
        masked_done = sem("masked_done")
        exp_done = sem("exp_done")
        inv_done = sem("inv_done")
        norm_done = sem("norm_done")
        turned = sem("turned")
        probsT_even = sem("probsT_even")
        probsT_odd = sem("probsT_odd")
        pv_done = sem("pv_done")
        attnT_done = sem("attnT_done")
        out_done = sem("out_done")
        y_done = sem("y_done")

        side_read = {"xT": xnT_done, "qk": qk_ready, "v": v_ready, "mix_rk": relu_done, "mix_v": gated_done}

        block = ctx.enter_context(nc.Block())
        SMALL_LOADS, WEIGHT_LOADS, CONSTS = 4, 4, 5
        BLOCK_COLS = [slice(0, P), slice(P, CAUSAL)]

        def wait(eng, signal, n):
            if not isinstance(n, int) or n > 0:
                eng.wait_ge(signal, n)

        def run(eng, slot_work, last=SLOTS + OUT_LAG):
            for c in range(START, TURN):
                slot_work(Slot(0, c))
            with eng.Fori(0, BATCHES - 1) as turn:
                for c in range(TURN, TURN + SLOTS):
                    slot_work(Slot(turn, c))
            for c in range(TURN, last + 1):
                slot_work(Slot(BATCHES - 1, c))

        def rows(first):
            return x[first, :].rearrange("(b p) e -> p b e", p=P)

        @block.sync
        def _(sync):
            sync.dma_start(x_in[:], rows(slice(0, TOKENS))).then_inc(x_in_loaded, 16)
            for n, heads in enumerate(CHUNKS):
                sync.dma_start(wqkv[:, heads, :], qkv_w[:, heads, :]).then_inc(qkv_w_in[n], 16)
            sync.dma_start(wr_sb[:], w_r).then_inc(weights_in, 16)
            sync.dma_start(wk_sb[:], w_k).then_inc(weights_in, 16)
            sync.dma_start(wv_sb[:], w_v).then_inc(weights_in, 16)
            sync.dma_start(wo[:], out_w.rearrange("(c p) e -> p c e", p=P)).then_inc(weights_in, 16)
            sync.dma_start(x_res[:], xT[:, 0:TOKENS]).then_inc(x_res_loaded, 16)
            sync.wait_ge(xn_done, 1)
            sync.dma_start(x_in[:], rows(slice(TOKENS, 2 * TOKENS))).then_inc(x_in_loaded, 16)

            def load_x(done, tokens):
                sync.wait_ge(xn_done, done)
                sync.dma_start(x_in[:], rows(tokens)).then_inc(x_in_loaded, 16)

            def load_residual(done, tokens):
                sync.wait_ge(residue_done, done)
                sync.dma_start(x_res[:], xT[:, tokens]).then_inc(x_res_loaded, 16)

            def store(done, tokens):
                sync.wait_ge(y_done, done)
                sync.dma_start(outT[:, tokens], y[:]).then_inc(y_free, 16)

            with sync.Fori(2, BATCHES) as b:
                load_x(b, bass.ds(b * TOKENS, TOKENS))
                load_residual(b - 1, bass.ds(b * TOKENS - TOKENS, TOKENS))
                store(b - 1, bass.ds(b * TOKENS - 2 * TOKENS, TOKENS))
            end = BATCHES * TOKENS
            load_residual(BATCHES - 1, slice(end - TOKENS, end))
            store(BATCHES - 1, slice(end - 2 * TOKENS, end - TOKENS))
            store(BATCHES, slice(end - TOKENS, end))
            sync.wait_ge(y_free, 16 * (BATCHES + 1))

        @block.gpsimd
        def _(pool):
            pool.memset(ident[:], 0.0).then_inc(mask_parts, 1)
            pool.memset(mask[:], 0.0).then_inc(mask_parts, 1)
            pool.memset(xnT[:, 0:1], 0.0).then_inc(mask_parts, 1)
            pool.memset(y[:], 0.0).then_inc(y_free, 16)
            pool.memset(rsqrt_exp[:], -0.5).then_inc(consts_ready, 1)
            pool.memset(eps[:], EPS).then_inc(consts_ready, 1)
            pool.wait_ge(mask_parts, 3)
            pool.affine_select(out=ident[:], in_=ident[:], compare_op=ALU.not_equal, fill=1.0, base=0,
                               pattern=[[-1, P]], channel_multiplier=1).then_inc(consts_ready, 1)
            for diagonal in (slice(0, P), slice(CAUSAL - P, CAUSAL)):
                pool.affine_select(out=mask[:, diagonal], in_=mask[:, diagonal], compare_op=ALU.is_ge,
                                   fill=MASKED, base=0, pattern=[[-1, P]],
                                   channel_multiplier=1).then_inc(consts_ready, 1)
            pool.wait_ge(consts_ready, CONSTS)

            def slot_work(s):
                last = s.back(1)
                if last.t in SIDE and SIDE[last.t][0] == "qk" and last.side_exists():
                    p = SIDE[last.t][1]
                    wait(pool, qk_hi_ready, last.side("qk"))
                    pool.tensor_tensor(qk_lo[:, p, :], qk[:, p, P:], qk_hi[:, p, :].bitcast(F32),
                                       ALU.subtract).then_inc(qk_lo_ready, 1)
                if s.t == 6 and s.batch(1):
                    wait(pool, mean_done, s.count(1, 2))
                    pool.tensor_tensor(var_eps[:], mean_var[:, :, 1], eps[:], ALU.add).then_inc(var_done, 1)
                    wait(pool, var_done, s.count(1, 2))
                    wait(pool, xn_done, s.count(1, 1))
                    pool.tensor_tensor(rstd[:], var_eps[:], rsqrt_exp[:], ALU.pow).then_inc(rstd_done, 1)
                if s.t == 10 and s.batch(1):
                    wait(pool, xnT_done, s.count(1, 2))
                    wait(pool, mix_done, s.count(1, 1))
                    pool.tensor_tensor(x_step[:], xnT[:, 1:], xnT[:, 0:TOKENS],
                                       ALU.subtract).then_inc(step_done, 1)
                if s.t == 4 and s.batch():
                    wait(pool, relu_done, s.count(1, 1))
                    pool.tensor_tensor(k_act[:], k_relu[:], k_relu[:], ALU.mult).then_inc(k_act_done, 1)

            run(pool, slot_work)

        @block.tensor
        def _(pe):
            pe.wait_ge(consts_ready, CONSTS)

            def split_product(out, weights, acts):
                parts = ((0, 0), (0, 1), (1, 0))
                for n, (a, b) in enumerate(parts):
                    mm = pe.matmul(out, weights[a], acts[b], start=(n == 0), stop=(n == len(parts) - 1))
                return mm

            def side_work(s):
                kind, *what = SIDE[s.t]
                out = ps_side[s.t % 2]
                ahead = s.t >= FIRST
                last = s.last_in_bank()
                if last.side_exists():
                    last_kind = SIDE[last.t][0]
                    wait(pe, side_read[last_kind], last.side(last_kind))
                if kind == "xT":
                    wait(pe, xn_done, s.count(1, 2))
                    for b in range(QB):
                        mm = pe.transpose(out[:, b * P:(b + 1) * P], xn[:, b, :], ident[:])
                elif kind == "qk":
                    if s.number() is not None and s.number() < TURN:
                        pe.wait_ge(weights_split, 3 * chunk_of(2 * what[0]) + 2)
                    wait(pe, xnT_split, s.count(1, 1 + ahead))
                    pair = slice(2 * what[0], 2 * what[0] + 2)
                    acts = (xnT_hi[:], xnT_lo[:])
                    split_product(out[:, 0:TOKENS], [w[:, pair, :] for w in wq], acts)
                    mm = split_product(out[:, TOKENS:2 * TOKENS], [w[:, pair, :] for w in wk], acts)
                elif kind == "v":
                    half, b = what
                    if s.number() is not None and s.number() < TURN:
                        pe.wait_ge(weights_split, 3 * chunk_of((half + 1) * PAIRS - 1) + 3)
                    wait(pe, xnT_split, s.count(1, 1 + ahead))
                    tokens = slice(b * P, (b + 1) * P)
                    heads = slice(half * PAIRS, (half + 1) * PAIRS)
                    mm = split_product(out[:], (xnT_hi[:, tokens], xnT_lo[:, tokens]),
                                       [w[:, heads, :] for w in wv])
                elif kind == "mix_rk":
                    wait(pe, mix_done, s.count(1, 1))
                    if s.number() == s.t:
                        pe.wait_ge(weights_in, 16 * WEIGHT_LOADS)
                    pe.matmul(out[:, 0:TOKENS], wr_sb[:], x_mix[:, 0, :], start=True, stop=True)
                    mm = pe.matmul(out[:, TOKENS:2 * TOKENS], wk_sb[:], x_mix[:, 1, :], start=True, stop=True)
                elif kind == "mix_v":
                    wait(pe, k_act_done, s.count(1, 1))
                    mm = pe.matmul(out[:, 0:TOKENS], wv_sb[:], k_act[:], start=True, stop=True)
                mm.then_inc(side_done[kind], 1)

            def slot_work(s):
                if s.batch():
                    pair, at = s.t // 2, slice(D * (s.t % 2), D * (s.t % 2) + D)
                    wait(pe, qk_lo_ready, s.pairs())
                    wait(pe, masked_done, s.back(2).heads())
                    out = ps_scores[s.t % 2]
                    pe.matmul(out[:, 0:P], qk[at, pair, 0:P], qk[at, pair, TOKENS:TOKENS + P],
                              start=True, stop=True)
                    split_product(out[:, P:CAUSAL], [part[at, pair, 0:P] for part in (qk_hi, qk_lo)],
                                  [part[at, pair, P:SPLIT] for part in (qk_hi, qk_lo)]).then_inc(scores_done, 1)
                if s.side_exists():
                    side_work(s)
                u = s.back(TURN_LAG)
                if u.batch():
                    wait(pe, norm_done, u.heads())
                    wait(pe, (probsT_even, probsT_odd)[u.t % 2], u.back(2).pairs())
                    for k in range(CAUSAL // P):
                        cols = slice(k * P, (k + 1) * P)
                        mm = pe.transpose(ps_turn[u.t % 2][:, cols], probs[:, u.t % 4, cols], ident[:])
                    mm.then_inc(turned, 1)
                u = s.back(PV_LAG)
                if u.batch() and u.t % 2:
                    wait(pe, probsT_even, u.pairs())
                    wait(pe, probsT_odd, u.pairs())
                    wait(pe, v_ready, u.count(4, 2 if u.t < PAIRS else 4))
                    wait(pe, attnT_done, u.back(2).pairs())
                    for k, (queries, cols) in enumerate(((slice(0, TOKENS), slice(0, TOKENS)),
                                                         (slice(P, TOKENS), slice(TOKENS, CAUSAL)))):
                        for n in range(2):
                            h = u.t - 1 + n
                            mm = pe.matmul(ps_attn[D * n:D * n + D, queries], v[:, k, h * D:(h + 1) * D],
                                           probsT[:, h % 4, cols], start=(k == 0), stop=(k == QB - 1))
                    mm.then_inc(pv_done, 1)
                u = s.back(OUT_LAG)
                if u.batch() and u.t % 2:
                    j = u.t // 2
                    wait(pe, attnT_done, u.pairs())
                    if j == 0:
                        wait(pe, y_done, u.count(1, 0))
                    pe.matmul(ps_out[:, 0:TOKENS], wo[:, j, :], attnT[:, j % 2, :],
                              start=(j == 0), stop=(j == PAIRS - 1)).then_inc(out_done, 1)

            run(pe, slot_work)

        @block.scalar
        def _(act):
            act.dma_start(bias[:], qkv_b).then_inc(small_in, 16)
            act.dma_start(mu[:, 0:1], mu_r).then_inc(small_in, 16)
            act.dma_start(mu[:, 1:2], mu_k).then_inc(small_in, 16)
            act.dma_start(bo[:], out_b).then_inc(small_in, 16)
            def upper_weights(c):
                heads = CHUNKS[c]
                act.wait_ge(qkv_w_in[c], 16)
                for n, w in enumerate((wq, wk, wv)):
                    act.copy(w[0][:, heads, :], wqkv[:, heads, n * D:(n + 1) * D]).then_inc(hi_ready, 1)

            def side_work(s):
                kind, *what = SIDE[s.t]
                out = ps_side[s.t % 2]
                if kind == "qk":
                    p = what[0]
                    wait(act, side_done["qk"], s.side("qk"))
                    for n, cols in enumerate((slice(0, TOKENS), slice(TOKENS, 2 * TOKENS))):
                        last = act.activation(qk[:, p, cols], out[:, cols], ACT.Identity, bias=bias[:, n, p:p + 1])
                    last.then_inc(qk_ready, 1)
                elif kind == "v":
                    half, b = what
                    wait(act, side_done["v"], s.side("v"))
                    act.copy(v[:, b, half * HALF:(half + 1) * HALF], out[:]).then_inc(v_ready, 1)
                elif kind == "xT":
                    wait(act, side_done["xT"], s.side("xT"))
                    wait(act, mix_done, s.count(1, 1))
                    wait(act, xnT_split, s.count(1, 1))
                    if s.number() is not None and s.number() < 0:
                        act.wait_ge(mask_parts, 3)
                    act.copy(xnT[:, 1:], out[:, 0:TOKENS]).then_inc(xnT_done, 1)
                elif kind == "mix_rk":
                    wait(act, side_done["mix_rk"], s.side("mix_rk"))
                    wait(act, gated_done, s.count(1, 0))
                    act.activation(r_tanh[:], out[:, 0:TOKENS], ACT.Tanh, scale=0.5)
                    act.activation(k_relu[:], out[:, TOKENS:2 * TOKENS],
                                   ACT.Relu).then_inc(relu_done, 1)

            def slot_work(s):
                u = s.back(OUT_LAG)
                if u.batch() and u.t % 2:
                    wait(act, pv_done, u.pairs())
                    act.activation(attnT[:, u.t // 2 % 2, :], ps_attn[:, 0:TOKENS], ACT.Identity,
                                   bias=bias[:, 2, u.t // 2:u.t // 2 + 1]).then_inc(attnT_done, 1)
                if s.side_exists():
                    side_work(s)
                u = s.back(TURN_LAG)
                if u.batch() and u.t % 2:
                    wait(act, turned, u.heads())
                    wait(act, pv_done, u.back(4).pairs())
                    act.copy(probsT[:, u.t % 4, :], ps_turn[1][:, 0:CAUSAL]).then_inc(probsT_odd, 1)
                if s.batch():
                    ring = s.t % 4
                    wait(act, masked_done, s.heads())
                    wait(act, turned, s.back(4).heads())
                    for b, cols in enumerate(BLOCK_COLS):
                        last = act.activation(probs[:, ring, cols], scores[:, s.t % 2, cols], ACT.Exp,
                                              bias=neg_top[:, ring, b:b + 1], scale=-1.0,
                                              accum_out=total[:, ring, b:b + 1])
                    last.then_inc(exp_done, 1)

                if s.number() in HI_AT:
                    upper_weights(HI_AT.index(s.number()))
                if s.number() == HI_AT[-1]:
                    act.wait_ge(small_in, 16 * SMALL_LOADS)

            run(act, slot_work)

        @block.vector
        def _(dve):
            def lower_weights(c):
                heads = CHUNKS[c]
                for n, w in enumerate((wq, wk, wv)):
                    dve.wait_ge(hi_ready, 3 * c + n + 1)
                    dve.tensor_tensor(w[1][:, heads, :], wqkv[:, heads, n * D:(n + 1) * D],
                                      w[0][:, heads, :].bitcast(F32), ALU.subtract).then_inc(weights_split, 1)


            def side_work(s):
                last = s.back(1)
                if last.t in SIDE and SIDE[last.t][0] == "qk" and last.side_exists():
                    p = SIDE[last.t][1]
                    wait(dve, qk_ready, last.side("qk"))
                    dve.tensor_copy(qk_hi[:, p, :], qk[:, p, P:]).then_inc(qk_hi_ready, 1)
                if s.t == 4 and s.batch(-1):
                    wait(dve, out_done, s.count(PAIRS, 0))
                    wait(dve, residue_done, s.count(1, 0))
                    wait(dve, y_free, s.count(16, 0))
                    dve.scalar_tensor_tensor(out=y[:], in0=ps_out[:, 0:TOKENS], scalar=bo[:, 0:1],
                                             in1=rest[:], op0=ALU.add, op1=ALU.add).then_inc(y_done, 1)
                if s.t == 5 and s.batch():
                    wait(dve, side_done["mix_v"], s.count(1, 1))
                    dve.scalar_tensor_tensor(out=gated[:], in0=r_tanh[:], scalar=1.0, in1=ps_side[1][:, 0:TOKENS],
                                             op0=ALU.add, op1=ALU.mult).then_inc(gated_done, 1)
                if s.t == 6 and s.batch(1):
                    wait(dve, x_in_loaded, s.count(16, 32))
                    for b in range(QB):
                        last = dve.bn_stats(stats[:, b, :], x_in[:, b, :])
                    last.then_inc(stats_done, 1)
                    wait(dve, stats_done, s.count(1, 2))
                    wait(dve, rstd_done, s.count(1, 1))
                    dve.memset(clear[:, 4:5], 0.0)
                    for b in range(QB):
                        last = dve.bn_aggr(mean_var[:, b, :], stats[:, b, :])
                    last.then_inc(mean_done, 1)
                if s.t == 7 and s.batch(1):
                    wait(dve, rstd_done, s.count(1, 2))
                    wait(dve, side_done["xT"], s.count(1, 1))
                    for b in range(QB):
                        last = dve.tensor_scalar(xn[:, b, :], x_in[:, b, :], mean_var[:, b, 0:1],
                                                 rstd[:, b:b + 1], ALU.subtract, ALU.mult)
                    last.then_inc(xn_done, 1)
                if s.t == 13 and s.batch():
                    wait(dve, gated_done, s.count(1, 1))
                    wait(dve, x_res_loaded, s.count(16, 16))
                    dve.scalar_tensor_tensor(out=rest[:], in0=gated[:], scalar=0.5, in1=x_res[:],
                                             op0=ALU.mult, op1=ALU.add).then_inc(residue_done, 1)
                if s.t == 9 and s.batch(1):
                    wait(dve, xnT_done, s.count(1, 2))
                    dve.tensor_copy(xnT_hi[:], xnT[:, 1:]).then_inc(xnT_hi_done, 1)
                    wait(dve, xnT_hi_done, s.count(1, 2))
                    dve.tensor_tensor(xnT_lo[:], xnT[:, 1:], xnT_hi[:].bitcast(F32),
                                      ALU.subtract).then_inc(xnT_split, 1)
                if s.t == 12 and s.batch(1):
                    wait(dve, step_done, s.count(1, 2))
                    wait(dve, side_done["mix_rk"], s.count(1, 1))
                    for n in range(2):
                        last = dve.scalar_tensor_tensor(out=x_mix[:, n, :], in0=x_step[:], scalar=mu[:, n:n + 1],
                                                        in1=xnT[:, 0:TOKENS], op0=ALU.mult, op1=ALU.add)
                    last.then_inc(mix_done, 1)

            def slot_work(s):
                if s.batch():
                    wait(dve, scores_done, s.heads())
                    wait(dve, exp_done, s.back(2).heads())
                    dve.memset(clear[:, s.t % 4:s.t % 4 + 1], 0.0)
                    for b, cols in enumerate(BLOCK_COLS):
                        last = dve.tensor_tensor_reduce(scores[:, s.t % 2, cols], ps_scores[s.t % 2][:, cols],
                                                        mask[:, cols], -D ** -0.5, HIGHEST, ALU.add, ALU.min,
                                                        neg_top[:, s.t % 4, b:b + 1])
                    last.then_inc(masked_done, 1)
                n = s.back(1)
                if n.batch():
                    wait(dve, exp_done, n.heads())
                    dve.reciprocal(inv_total[:, n.t % 4, :], total[:, n.t % 4, :]).then_inc(inv_done, 1)
                u = s.back(TURN_LAG)
                if u.batch() and u.t % 2 == 0:
                    wait(dve, turned, u.heads())
                    wait(dve, pv_done, u.back(4).pairs())
                    dve.tensor_copy(probsT[:, u.t % 4, :], ps_turn[0][:, 0:CAUSAL]).then_inc(probsT_even, 1)
                if n.batch():
                    wait(dve, inv_done, n.heads())
                    for b, cols in enumerate(BLOCK_COLS):
                        block_probs = probs[:, n.t % 4, cols]
                        last = dve.tensor_scalar(block_probs, block_probs, inv_total[:, n.t % 4, b:b + 1], None,
                                                 ALU.mult)
                    last.then_inc(norm_done, 1)
                side_work(s)
                if s.number() in LO_AT:
                    lower_weights(LO_AT.index(s.number()))
                if s.number() == LO_AT[1]:
                    dve.wait_ge(small_in, 16 * SMALL_LOADS)
                    dve.wait_ge(consts_ready, CONSTS)

            run(dve, slot_work)


def kernel(L0_attn_x, L0_attn_qkv_w, L0_attn_qkv_b, L0_attn_out_w, L0_attn_out_b,
           L0_ffn_W_r, L0_ffn_W_k, L0_ffn_W_v, L0_ffn_mu_r, L0_ffn_mu_k):
    import numpy as np
    from concourse import bacc
    from concourse.bass_utils import run_bass_kernel_spmd

    flat = np.asarray(L0_attn_x).reshape(BATCHES * TOKENS, E)
    by_pair = np.asarray(L0_attn_qkv_b).reshape(PAIRS, 2, 3, D).transpose(1, 3, 2, 0).reshape(P, 3, PAIRS)
    arrays = {
        "x": flat, "xT": flat.T, "qkv_w": L0_attn_qkv_w, "qkv_b": by_pair,
        "out_w": np.asarray(L0_attn_out_w).reshape(HEADS * D, E), "out_b": np.asarray(L0_attn_out_b).reshape(E, 1),
        "w_r": np.asarray(L0_ffn_W_r).T, "w_k": np.asarray(L0_ffn_W_k).T, "w_v": np.asarray(L0_ffn_W_v).T,
        "mu_r": np.asarray(L0_ffn_mu_r).reshape(E, 1), "mu_k": np.asarray(L0_ffn_mu_k).reshape(E, 1),
    }
    arrays = {name: np.ascontiguousarray(a) for name, a in arrays.items()}
    nc = bacc.Bacc("TRN2", target_bir_lowering=False, num_devices=1)
    args = [nc.dram_tensor(name, a.shape, F32, kind="ExternalInput").ap() for name, a in arrays.items()]
    outT = nc.dram_tensor("outT", (E, BATCHES * TOKENS), F32, kind="ExternalOutput").ap()
    build(nc, *args, outT)
    r = run_bass_kernel_spmd(nc, [arrays], core_ids=[0])
    return np.ascontiguousarray(r.results[0]["outT"].T).reshape(BATCHES, TOKENS, E)
```

```python
from contextlib import ExitStack

import concourse.bass as bass
from concourse import mybir

ALU = mybir.AluOpType
ACT = mybir.ActivationFunctionType
F32 = mybir.dt.float32
F32R = mybir.dt.float32r

P = 128
BATCHES, TOKENS, E = 16, 256, 128
HEADS, D = 16, 64
PAIRS = HEADS // 2
QB = TOKENS // P
SPLIT = P + TOKENS
CAUSAL = P + TOKENS
HALF = HEADS * D // 2
EPS = 1e-5
MASKED = -0.7 * 3.4028234663852886e38
HIGHEST = 3.4e38

SLOTS = HEADS
ACT_TURN, DVE_TURN, POOL_TURN, PE_TURN, SP_TURN = 6, 5, 5, 7, 1
TURN_LAG, PV_LAG, ATTN_LAG, OUT_LAG = 3, 4, 5, 7

SIDE = {0: ("qk", 4), 1: ("mix_rk",), 2: ("qk", 5), 3: ("qk", 6), 4: ("mix_v",), 5: ("v", 1, 0),
        6: ("qk", 7), 7: ("v", 1, 1), 8: ("xT",), 9: ("qk", 0), 10: ("qk", 1), 11: ("qk", 2),
        13: ("qk", 3), 14: ("v", 0, 0), 15: ("v", 0, 1)}
PARTS = {1: 4, 3: 5, 4: 6, 7: 7, 10: 0, 11: 1, 12: 2, 14: 3}
LATE = (9,)
KINDS = {s[0] for s in SIDE.values()}
FIRST = 8
START = 5 - SLOTS

HALVES = (slice(0, D), slice(D, P))
GROUP = 2
STACKED = 6 * 16
CHUNKS = (slice(0, 4), slice(4, 8), slice(8, 16))
HI_AT = (-10, -9, -8)
LO_AT = (-9, -8, -5)
WO_AT = -3


def chunk_of(head):
    return next(n for n, heads in enumerate(CHUNKS) if head < heads.stop)


class Slot:

    def __init__(self, turn, c):
        self.turn, self.c = turn, c
        self.t = c % SLOTS

    def back(self, n):
        return Slot(self.turn, self.c - n)

    def number(self):
        return self.turn * SLOTS + self.c if isinstance(self.turn, int) else None

    def batch(self, ahead=0):
        n = self.number()
        return n is None or 0 <= n // SLOTS + ahead < BATCHES

    def side_exists(self):
        return self.t in SIDE and self.batch(self.t >= FIRST)

    def count(self, per_window, so_far):
        return self.turn * per_window + (self.c // SLOTS) * per_window + so_far

    def heads(self):
        return self.count(SLOTS, self.t + 1)

    def pairs(self):
        return self.count(PAIRS, self.t // 2 + 1)

    def side(self, kind):
        slots = [s for s, what in SIDE.items() if what[0] == kind]
        return self.count(len(slots), sum(s >= FIRST for s in slots) + sum(s <= self.t for s in slots))

    def split_pairs(self):
        return self.count(PAIRS - 1, self.t // 2 + 1)

    def parts_of(self):
        pair = PARTS.get(self.t)
        return pair if pair is not None and self.batch(pair < PAIRS // 2) else None

    def parts(self):
        pair = PARTS[self.t]
        return self.count(PAIRS, PAIRS * (pair < PAIRS // 2) + pair + 1)

    def last_in_bank(self):
        return next(s for s in (self.back(n) for n in range(2, SLOTS, 2)) if s.t in SIDE)


def build(nc, x, xT, qkv_w, qkv_b, out_w, out_b, w_r, w_k, w_v, mu_r, mu_k, outT):
    with ExitStack() as ctx:
        def sb(name, shape, dt=F32):
            return ctx.enter_context(nc.sbuf_tensor(name, shape, dt))

        def bank(name):
            return ctx.enter_context(nc.psum_tensor(name, [P, 512], F32))

        def sem(name):
            return ctx.enter_context(nc.semaphore(name))

        wqkv = sb("wqkv", [E, HEADS, 3 * D])
        wq = [sb("wq_hi", [E, HEADS, D], F32R), sb("wq_lo", [E, HEADS, D], F32R)]
        wk = [sb("wk_hi", [E, HEADS, D], F32R), sb("wk_lo", [E, HEADS, D], F32R)]
        wv = [sb("wv_hi", [E, HEADS, D], F32R), sb("wv_lo", [E, HEADS, D], F32R)]
        bias = sb("bias", [P, 3, PAIRS])
        wo = sb("wo", [P, PAIRS, E])
        wo_parts = [sb("wo_hi", [P, PAIRS, E], F32R), sb("wo_lo", [P, PAIRS, E], F32R)]
        bo = sb("bo", [E, 1])
        wr_sb, wk_sb, wv_sb = sb("mix_wr", [E, E]), sb("mix_wk", [E, E]), sb("mix_wv", [E, E])
        mu = sb("mu", [E, 2])
        ident = sb("ident", [P, P])
        mask = sb("mask", [P, CAUSAL])
        rsqrt_exp = sb("rsqrt_exp", [P, QB])
        eps = sb("eps", [P, QB])
        clear = sb("clear", [P, 5])

        x_in = sb("x_in", [P, QB, E])
        stats = sb("stats", [P, QB, 6])
        mean_var = sb("mean_var", [P, QB, 2])
        var_eps = sb("var_eps", [P, QB])
        rstd = sb("rstd", [P, QB])
        centred = sb("centred", [P, QB, E])
        xn = sb("xn", [P, QB, E])
        xnT = sb("xnT", [E, 1 + TOKENS])
        xnT_hi, xnT_lo = sb("xnT_hi", [E, TOKENS], F32R), sb("xnT_lo", [E, TOKENS], F32R)
        qk = sb("qk", [P, PAIRS, 2 * TOKENS])
        qk_hi, qk_lo = sb("qk_hi", [P, PAIRS, SPLIT], F32R), sb("qk_lo", [P, PAIRS, SPLIT], F32R)
        stack = sb("stack", [P, HEADS, SPLIT], F32R)
        v = sb("v", [P, QB, HEADS * D])
        x_res = sb("x_res", [E, TOKENS])
        x_step = sb("x_step", [E, TOKENS])
        x_mix = sb("x_mix", [E, 2, TOKENS])
        r_tanh = sb("r_tanh", [E, TOKENS])
        k_relu = sb("k_relu", [E, TOKENS])
        k_act = sb("k_act", [E, TOKENS])
        gated = sb("gated", [E, TOKENS])
        rest = sb("rest", [E, TOKENS])
        y = sb("y", [E, TOKENS])

        scores = sb("scores", [P, 2, CAUSAL])
        neg_top = sb("neg_top", [P, 4, QB])
        probs = sb("probs", [P, 4, CAUSAL])
        total = sb("total", [P, 4, QB])
        inv_total = sb("inv_total", [P, 4, QB])
        probsT = sb("probsT", [P, 4, CAUSAL])
        attnT = sb("attnT", [P, 2, TOKENS])
        attnT_hi, attnT_lo = sb("attnT_hi", [P, 2, TOKENS], F32R), sb("attnT_lo", [P, 2, TOKENS], F32R)

        ps_scores = [bank("ps_scores0"), bank("ps_scores1")]
        ps_turn = [bank("ps_turn0"), bank("ps_turn1")]
        ps_attn = bank("ps_attn")
        ps_out = bank("ps_out")
        ps_side = [bank("ps_side0"), bank("ps_side1")]

        qkv_w_in = [sem(f"qkv_w_in{n}") for n in range(len(CHUNKS))]
        small_in = sem("small_in")
        weights_in = sem("weights_in")
        x_in_loaded = sem("x_in_loaded")
        x_res_loaded = sem("x_res_loaded")
        y_free = sem("y_free")
        mask_parts = sem("mask_parts")
        consts_ready = sem("consts_ready")
        hi_ready = sem("hi_ready")
        weights_split = sem("weights_split")
        stats_done = sem("stats_done")
        mean_done = sem("mean_done")
        var_done = sem("var_done")
        rstd_done = sem("rstd_done")
        centred_done = sem("centred_done")
        xn_done = sem("xn_done")
        xnT_done = sem("xnT_done")
        xnT_hi_done = sem("xnT_hi_done")
        xnT_split = sem("xnT_split")
        side_done = {k: sem(f"side_{k}_done") for k in sorted(KINDS)}
        qk_ready = sem("qk_ready")
        qk_hi_ready = sem("qk_hi_ready")
        qk_lo_ready = sem("qk_lo_ready")
        stacked = [sem(f"stacked{n}") for n in range(PAIRS // GROUP)]
        v_ready = sem("v_ready")
        step_done = sem("step_done")
        mix_done = sem("mix_done")
        relu_done = sem("relu_done")
        k_act_done = sem("k_act_done")
        gated_done = sem("gated_done")
        residue_done = sem("residue_done")
        scores_done = sem("scores_done")
        masked_done = sem("masked_done")
        exp_done = sem("exp_done")
        inv_done = sem("inv_done")
        norm_done = sem("norm_done")
        turned = sem("turned")
        probsT_even = sem("probsT_even")
        probsT_odd = sem("probsT_odd")
        pv_done = sem("pv_done")
        attnT_done = sem("attnT_done")
        attnT_hi_done = sem("attnT_hi_done")
        attnT_lo_done = sem("attnT_lo_done")
        wo_hi_done = sem("wo_hi_done")
        wo_lo_done = sem("wo_lo_done")
        out_done = sem("out_done")
        y_done = sem("y_done")

        side_read = {"xT": xnT_hi_done, "qk": qk_ready, "v": v_ready, "mix_rk": relu_done, "mix_v": gated_done}

        block = ctx.enter_context(nc.Block())
        SMALL_LOADS, WEIGHT_LOADS, CONSTS = 4, 4, 5
        BLOCK_COLS = [slice(0, P), slice(P, CAUSAL)]

        def wait(eng, signal, n):
            if not isinstance(n, int) or n > 0:
                eng.wait_ge(signal, n)

        def run(eng, slot_work, turn_at, last=SLOTS + OUT_LAG):
            for c in range(START, turn_at):
                slot_work(Slot(0, c))
            with eng.Fori(0, BATCHES - 1) as turn:
                for c in range(turn_at, turn_at + SLOTS):
                    slot_work(Slot(turn, c))
            for c in range(turn_at, last + 1):
                slot_work(Slot(BATCHES - 1, c))

        def tokens(first):
            return slice(first, first + TOKENS) if isinstance(first, int) else bass.ds(first, TOKENS)

        def columns(s, ahead):
            return tokens((s.turn + (s.c // SLOTS + ahead)) * TOKENS)

        def rows(s, ahead):
            first = s.turn * TOKENS + (s.c // SLOTS + ahead) * TOKENS
            return x[tokens(first), :].rearrange("(b p) e -> p b e", p=P)

        @block.sync
        def _(sync):
            def load_weights():
                for n, heads in enumerate(CHUNKS):
                    sync.dma_start(wqkv[:, heads, :], qkv_w[:, heads, :]).then_inc(qkv_w_in[n], 16)
                sync.dma_start(wr_sb[:], w_r).then_inc(weights_in, 16)
                sync.dma_start(wk_sb[:], w_k).then_inc(weights_in, 16)
                sync.dma_start(wv_sb[:], w_v).then_inc(weights_in, 16)
                sync.dma_start(wo[:], out_w.rearrange("(c p) e -> p c e", p=P)).then_inc(weights_in, 16)

            stacked_as, hi, lo = stack[:].bitcast(F32), qk_hi[:].bitcast(F32), qk_lo[:].bitcast(F32)

            def slot_work(s):
                p = s.parts_of()
                if p is not None and p % GROUP == GROUP - 1:
                    pairs = slice(p + 1 - GROUP, p + 1)
                    moved = stacked[p // GROUP]
                    wait(sync, qk_hi_ready, s.parts())
                    for n, (own, other) in enumerate((HALVES, HALVES[::-1])):
                        heads = slice(2 * pairs.start + n, 2 * pairs.stop, 2)
                        sync.dma_start(stacked_as[own, heads, :], hi[own, pairs, :]).then_inc(moved, 16)
                        sync.dma_start(stacked_as[other, heads, 0:P], hi[own, pairs, 0:P]).then_inc(moved, 16)
                    wait(sync, qk_lo_ready, s.parts())
                    for n, (own, other) in enumerate((HALVES, HALVES[::-1])):
                        heads = slice(2 * pairs.start + n, 2 * pairs.stop, 2)
                        sync.dma_start(stacked_as[other, heads, P:], lo[own, pairs, P:]).then_inc(moved, 16)
                if s.t == 1 and s.batch(1):
                    wait(sync, xn_done, s.count(1, 1))
                    sync.dma_start(x_in[:], rows(s, 1)).then_inc(x_in_loaded, 16)
                if s.t == 14 and s.batch(1):
                    wait(sync, residue_done, s.count(1, 1))
                    sync.dma_start(x_res[:], xT[:, columns(s, 1)]).then_inc(x_res_loaded, 16)

            sync.dma_start(x_in[:], rows(Slot(0, START), 1)).then_inc(x_in_loaded, 16)
            load_weights()
            run(sync, slot_work, SP_TURN)
            sync.wait_ge(y_free, 16 * (BATCHES + 1))

        @block.gpsimd
        def _(pool):
            pool.memset(ident[:], 0.0).then_inc(mask_parts, 1)
            pool.memset(mask[:], 0.0).then_inc(mask_parts, 1)
            pool.memset(xnT[:, 0:1], 0.0).then_inc(mask_parts, 1)
            pool.memset(y[:], 0.0).then_inc(y_free, 16)
            pool.memset(rsqrt_exp[:], -0.5).then_inc(consts_ready, 1)
            pool.memset(eps[:], EPS).then_inc(consts_ready, 1)
            pool.wait_ge(mask_parts, 3)
            pool.affine_select(out=ident[:], in_=ident[:], compare_op=ALU.not_equal, fill=1.0, base=0,
                               pattern=[[-1, P]], channel_multiplier=1).then_inc(consts_ready, 1)
            for diagonal in (slice(0, P), slice(CAUSAL - P, CAUSAL)):
                pool.affine_select(out=mask[:, diagonal], in_=mask[:, diagonal], compare_op=ALU.is_ge,
                                   fill=MASKED, base=0, pattern=[[-1, P]],
                                   channel_multiplier=1).then_inc(consts_ready, 1)
            pool.wait_ge(consts_ready, CONSTS)

            def slot_work(s):
                u = s.back(ATTN_LAG)
                if u.batch() and u.t % 2 and u.t < HEADS - 1:
                    j = u.t // 2 % 2
                    wait(pool, attnT_hi_done, u.split_pairs())
                    pool.tensor_tensor(attnT_lo[:, j, :], attnT[:, j, :], attnT_hi[:, j, :].bitcast(F32),
                                       ALU.subtract).then_inc(attnT_lo_done, 1)
                if s.number() == WO_AT:
                    pool.wait_ge(wo_hi_done, 1)
                    pool.tensor_tensor(wo_parts[1][:], wo[:], wo_parts[0][:].bitcast(F32),
                                       ALU.subtract).then_inc(wo_lo_done, 1)
                p = s.parts_of()
                if p is not None:
                    wait(pool, qk_hi_ready, s.parts())
                    pool.tensor_tensor(qk_lo[:, p, :], qk[:, p, P:], qk_hi[:, p, :].bitcast(F32),
                                       ALU.subtract).then_inc(qk_lo_ready, 1)
                if s.t == 5 and s.batch(1):
                    wait(pool, mean_done, s.count(1, 2))
                    pool.tensor_tensor(var_eps[:], mean_var[:, :, 1], eps[:], ALU.add).then_inc(var_done, 1)
                    wait(pool, var_done, s.count(1, 2))
                    wait(pool, xn_done, s.count(1, 1))
                    pool.tensor_tensor(rstd[:], var_eps[:], rsqrt_exp[:], ALU.pow).then_inc(rstd_done, 1)
                    wait(pool, side_done["xT"], s.count(1, 1))
                    pool.tensor_tensor(centred[:], x_in[:], mean_var[:, :, 0:1].to_broadcast([P, QB, E]),
                                       ALU.subtract).then_inc(centred_done, 1)
                    wait(pool, rstd_done, s.count(1, 2))
                    wait(pool, centred_done, s.count(1, 2))
                    pool.tensor_tensor(xn[:], centred[:], rstd[:, :, None].to_broadcast([P, QB, E]),
                                       ALU.mult).then_inc(xn_done, 1)
                if s.t == 9 and s.batch(1):
                    wait(pool, xnT_done, s.count(1, 2))
                    wait(pool, mix_done, s.count(1, 1))
                    pool.tensor_tensor(x_step[:], xnT[:, 1:], xnT[:, 0:TOKENS],
                                       ALU.subtract).then_inc(step_done, 1)
                if s.t == 2 and s.batch():
                    wait(pool, relu_done, s.count(1, 1))
                    pool.tensor_tensor(k_act[:], k_relu[:], k_relu[:], ALU.mult).then_inc(k_act_done, 1)

            run(pool, slot_work, POOL_TURN)

        @block.tensor
        def _(pe):
            pe.wait_ge(consts_ready, CONSTS)

            def split_product(out, weights, acts, first=True, last=True):
                parts = ((0, 0), (0, 1), (1, 0))
                for n, (a, b) in enumerate(parts):
                    mm = pe.matmul(out, weights[a], acts[b], start=(first and n == 0),
                                   stop=(last and n == len(parts) - 1))
                return mm

            def side_work(s):
                kind, *what = SIDE[s.t]
                out = ps_side[s.t % 2]
                ahead = s.t >= FIRST
                last = s.last_in_bank()
                if last.side_exists():
                    last_kind = SIDE[last.t][0]
                    wait(pe, side_read[last_kind], last.side(last_kind))
                if kind == "xT":
                    wait(pe, xn_done, s.count(1, 2))
                    for b in range(QB):
                        mm = pe.transpose(out[:, b * P:(b + 1) * P], xn[:, b, :], ident[:])
                elif kind == "qk":
                    if s.number() is not None and s.number() < PE_TURN:
                        pe.wait_ge(weights_split, 3 * chunk_of(2 * what[0]) + 2)
                    wait(pe, xnT_split, s.count(1, 1 + ahead))
                    pair = slice(2 * what[0], 2 * what[0] + 2)
                    acts = (xnT_hi[:], xnT_lo[:])
                    split_product(out[:, 0:TOKENS], [w[:, pair, :] for w in wq], acts)
                    mm = split_product(out[:, TOKENS:2 * TOKENS], [w[:, pair, :] for w in wk], acts)
                elif kind == "v":
                    half, b = what
                    if s.number() is not None and s.number() < PE_TURN:
                        pe.wait_ge(weights_split, 3 * chunk_of((half + 1) * PAIRS - 1) + 3)
                    wait(pe, xnT_split, s.count(1, 1 + ahead))
                    tokens = slice(b * P, (b + 1) * P)
                    heads = slice(half * PAIRS, (half + 1) * PAIRS)
                    mm = split_product(out[:], (xnT_hi[:, tokens], xnT_lo[:, tokens]),
                                       [w[:, heads, :] for w in wv])
                elif kind == "mix_rk":
                    wait(pe, mix_done, s.count(1, 1))
                    if s.number() == s.t:
                        pe.wait_ge(weights_in, 16 * WEIGHT_LOADS)
                    pe.matmul(out[:, 0:TOKENS], wr_sb[:], x_mix[:, 0, :], start=True, stop=True)
                    mm = pe.matmul(out[:, TOKENS:2 * TOKENS], wk_sb[:], x_mix[:, 1, :], start=True, stop=True)
                elif kind == "mix_v":
                    wait(pe, k_act_done, s.count(1, 1))
                    mm = pe.matmul(out[:, 0:TOKENS], wv_sb[:], k_act[:], start=True, stop=True)
                mm.then_inc(side_done[kind], 1)

            def slot_work(s):
                if s.batch():
                    pair, at = s.t // 2, HALVES[s.t % 2]
                    wait(pe, stacked[pair // GROUP], s.count(STACKED, STACKED))
                    wait(pe, masked_done, s.back(2).heads())
                    out = ps_scores[s.t % 2]
                    pe.matmul(out[:, 0:P], qk[at, pair, 0:P], qk[at, pair, TOKENS:TOKENS + P],
                              start=True, stop=True)
                    pe.matmul(out[:, P:CAUSAL], stack[:, s.t, 0:P], stack[:, s.t, P:], start=True, stop=False)
                    pe.matmul(out[:, P:CAUSAL], qk_lo[at, pair, 0:P], qk_hi[at, pair, P:],
                              start=False, stop=True).then_inc(scores_done, 1)
                if s.side_exists() and s.t not in LATE:
                    side_work(s)
                if s.t == 6 and s.batch(-1):
                    wait(pe, y_done, s.count(1, 0))
                u = s.back(OUT_LAG)
                if u.batch() and u.t % 2 and u.t < HEADS - 1:
                    j = u.t // 2
                    wait(pe, attnT_lo_done, u.split_pairs())
                    if u.number() == 1:
                        pe.wait_ge(wo_lo_done, 1)
                    split_product(ps_out[:, 0:TOKENS], [w[:, j, :] for w in wo_parts],
                                  (attnT_hi[:, j % 2, :], attnT_lo[:, j % 2, :]),
                                  first=(j == 0), last=False)
                u = s.back(TURN_LAG)
                if u.batch():
                    wait(pe, norm_done, u.heads())
                    wait(pe, (probsT_even, probsT_odd)[u.t % 2], u.back(2).pairs())
                    for k in range(CAUSAL // P):
                        cols = slice(k * P, (k + 1) * P)
                        mm = pe.transpose(ps_turn[u.t % 2][:, cols], probs[:, u.t % 4, cols], ident[:])
                    mm.then_inc(turned, 1)
                u = s.back(PV_LAG)
                if u.batch() and u.t % 2:
                    wait(pe, probsT_even, u.pairs())
                    wait(pe, probsT_odd, u.pairs())
                    wait(pe, v_ready, u.count(4, 2 if u.t < PAIRS else 4))
                    wait(pe, attnT_done, u.back(2).pairs())
                    for k, (queries, cols) in enumerate(((slice(0, TOKENS), slice(0, TOKENS)),
                                                         (slice(P, TOKENS), slice(TOKENS, CAUSAL)))):
                        for n in range(2):
                            h = u.t - 1 + n
                            mm = pe.matmul(ps_attn[D * n:D * n + D, queries], v[:, k, h * D:(h + 1) * D],
                                           probsT[:, h % 4, cols], start=(k == 0), stop=(k == QB - 1))
                    mm.then_inc(pv_done, 1)
                u = s.back(ATTN_LAG)
                if u.batch() and u.t == HEADS - 1:
                    wait(pe, attnT_done, u.pairs())
                    pe.matmul(ps_out[:, 0:TOKENS], wo[:, PAIRS - 1, :], attnT[:, (PAIRS - 1) % 2, :],
                              start=False, stop=True).then_inc(out_done, 1)
                if s.side_exists() and s.t in LATE:
                    side_work(s)

            run(pe, slot_work, PE_TURN)

        @block.scalar
        def _(act):
            act.dma_start(bias[:], qkv_b).then_inc(small_in, 16)
            act.dma_start(mu[:, 0:1], mu_r).then_inc(small_in, 16)
            act.dma_start(mu[:, 1:2], mu_k).then_inc(small_in, 16)
            act.dma_start(bo[:], out_b).then_inc(small_in, 16)

            def upper_weights(c):
                heads = CHUNKS[c]
                act.wait_ge(qkv_w_in[c], 16)
                for n, w in enumerate((wq, wk, wv)):
                    act.copy(w[0][:, heads, :], wqkv[:, heads, n * D:(n + 1) * D]).then_inc(hi_ready, 1)

            def side_work(s):
                kind, *what = SIDE[s.t]
                out = ps_side[s.t % 2]
                if kind == "qk":
                    p = what[0]
                    wait(act, side_done["qk"], s.side("qk"))
                    for n, cols in enumerate((slice(0, TOKENS), slice(TOKENS, 2 * TOKENS))):
                        last = act.activation(qk[:, p, cols], out[:, cols], ACT.Identity, bias=bias[:, n, p:p + 1])
                    last.then_inc(qk_ready, 1)
                elif kind == "v":
                    half, b = what
                    wait(act, side_done["v"], s.side("v"))
                    act.copy(v[:, b, half * HALF:(half + 1) * HALF], out[:]).then_inc(v_ready, 1)
                elif kind == "xT":
                    wait(act, side_done["xT"], s.side("xT"))
                    wait(act, mix_done, s.count(1, 1))
                    wait(act, xnT_split, s.count(1, 1))
                    if s.number() is not None and s.number() < 0:
                        act.wait_ge(mask_parts, 3)
                    act.copy(xnT[:, 1:], out[:, 0:TOKENS]).then_inc(xnT_done, 1)
                    act.copy(xnT_hi[:], out[:, 0:TOKENS]).then_inc(xnT_hi_done, 1)
                elif kind == "mix_rk":
                    wait(act, side_done["mix_rk"], s.side("mix_rk"))
                    wait(act, gated_done, s.count(1, 0))
                    act.activation(r_tanh[:], out[:, 0:TOKENS], ACT.Tanh, scale=0.5)
                    act.activation(k_relu[:], out[:, TOKENS:2 * TOKENS],
                                   ACT.Relu).then_inc(relu_done, 1)

            def slot_work(s):
                u = s.back(ATTN_LAG)
                if u.batch() and u.t % 2:
                    wait(act, pv_done, u.pairs())
                    act.activation(attnT[:, u.t // 2 % 2, :], ps_attn[:, 0:TOKENS], ACT.Identity,
                                   bias=bias[:, 2, u.t // 2:u.t // 2 + 1]).then_inc(attnT_done, 1)
                if s.side_exists() and s.t not in LATE:
                    side_work(s)
                u = s.back(TURN_LAG)
                if u.batch() and u.t % 2:
                    wait(act, turned, u.heads())
                    act.copy(probsT[:, u.t % 4, :], ps_turn[1][:, 0:CAUSAL]).then_inc(probsT_odd, 1)
                if s.batch():
                    ring = s.t % 4
                    wait(act, masked_done, s.heads())
                    wait(act, turned, s.back(4).heads())
                    for b, cols in enumerate(BLOCK_COLS):
                        last = act.activation(probs[:, ring, cols], scores[:, s.t % 2, cols], ACT.Exp,
                                              bias=neg_top[:, ring, b:b + 1], scale=-1.0,
                                              accum_out=total[:, ring, b:b + 1])
                    last.then_inc(exp_done, 1)
                if s.side_exists() and s.t in LATE:
                    side_work(s)
                if s.t == 5 and s.batch(-1):
                    wait(act, y_done, s.count(1, 0))
                    act.dma_start(outT[:, columns(s, -1)], y[:]).then_inc(y_free, 16)
                if s.number() == WO_AT:
                    act.wait_ge(weights_in, 16 * WEIGHT_LOADS)
                    act.copy(wo_parts[0][:], wo[:]).then_inc(wo_hi_done, 1)
                if s.number() in HI_AT:
                    upper_weights(HI_AT.index(s.number()))
                if s.number() == FIRST - SLOTS:
                    act.wait_ge(small_in, 16 * SMALL_LOADS)

            run(act, slot_work, ACT_TURN)

        @block.vector
        def _(dve):
            def lower_weights(c):
                heads = CHUNKS[c]
                for n, w in enumerate((wq, wk, wv)):
                    dve.wait_ge(hi_ready, 3 * c + n + 1)
                    dve.tensor_tensor(w[1][:, heads, :], wqkv[:, heads, n * D:(n + 1) * D],
                                      w[0][:, heads, :].bitcast(F32), ALU.subtract).then_inc(weights_split, 1)

            def side_work(s):
                p = s.parts_of()
                if p is not None:
                    wait(dve, qk_ready, s.parts())
                    dve.tensor_copy(qk_hi[:, p, :], qk[:, p, P:]).then_inc(qk_hi_ready, 1)
                u = s.back(ATTN_LAG)
                if u.batch() and u.t % 2 and u.t < HEADS - 1:
                    wait(dve, attnT_done, u.pairs())
                    dve.tensor_copy(attnT_hi[:, u.t // 2 % 2, :], attnT[:, u.t // 2 % 2, :]).then_inc(attnT_hi_done, 1)
                if s.t == 4 and s.batch(-1):
                    wait(dve, out_done, s.count(1, 0))
                    wait(dve, residue_done, s.count(1, 0))
                    wait(dve, y_free, s.count(16, 0))
                    dve.scalar_tensor_tensor(out=y[:], in0=ps_out[:, 0:TOKENS], scalar=bo[:, 0:1],
                                             in1=rest[:], op0=ALU.add, op1=ALU.add).then_inc(y_done, 1)
                if s.t == 4 and s.batch():
                    wait(dve, side_done["mix_v"], s.count(1, 1))
                    wait(dve, residue_done, s.count(1, 0))
                    dve.scalar_tensor_tensor(out=gated[:], in0=r_tanh[:], scalar=1.0, in1=ps_side[0][:, 0:TOKENS],
                                             op0=ALU.add, op1=ALU.mult).then_inc(gated_done, 1)
                if s.t == 5 and s.batch(1):
                    wait(dve, x_in_loaded, s.count(16, 32))
                    for b in range(QB):
                        last = dve.bn_stats(stats[:, b, :], x_in[:, b, :])
                    last.then_inc(stats_done, 1)
                    wait(dve, stats_done, s.count(1, 2))
                    wait(dve, xn_done, s.count(1, 1))
                    dve.memset(clear[:, 4:5], 0.0)
                    for b in range(QB):
                        last = dve.bn_aggr(mean_var[:, b, :], stats[:, b, :])
                    last.then_inc(mean_done, 1)
                if s.t == 13 and s.batch():
                    wait(dve, gated_done, s.count(1, 1))
                    wait(dve, x_res_loaded, s.count(16, 16))
                    dve.scalar_tensor_tensor(out=rest[:], in0=gated[:], scalar=0.5, in1=x_res[:],
                                             op0=ALU.mult, op1=ALU.add).then_inc(residue_done, 1)
                if s.t == 8 and s.batch(1):
                    wait(dve, xnT_hi_done, s.count(1, 2))
                    dve.tensor_tensor(xnT_lo[:], xnT[:, 1:], xnT_hi[:].bitcast(F32),
                                      ALU.subtract).then_inc(xnT_split, 1)
                if s.t == 14 and s.batch(1):
                    wait(dve, step_done, s.count(1, 2))
                    wait(dve, side_done["mix_rk"], s.count(1, 1))
                    for n in range(2):
                        last = dve.scalar_tensor_tensor(out=x_mix[:, n, :], in0=x_step[:], scalar=mu[:, n:n + 1],
                                                        in1=xnT[:, 0:TOKENS], op0=ALU.mult, op1=ALU.add)
                    last.then_inc(mix_done, 1)

            def slot_work(s):
                if s.batch():
                    wait(dve, scores_done, s.heads())
                    wait(dve, exp_done, s.back(2).heads())
                    dve.memset(clear[:, s.t % 4:s.t % 4 + 1], 0.0)
                    for b, cols in enumerate(BLOCK_COLS):
                        last = dve.tensor_tensor_reduce(scores[:, s.t % 2, cols], ps_scores[s.t % 2][:, cols],
                                                        mask[:, cols], -D ** -0.5, HIGHEST, ALU.add, ALU.min,
                                                        neg_top[:, s.t % 4, b:b + 1])
                    last.then_inc(masked_done, 1)
                n = s.back(1)
                if n.batch():
                    wait(dve, exp_done, n.heads())
                    dve.reciprocal(inv_total[:, n.t % 4, :], total[:, n.t % 4, :]).then_inc(inv_done, 1)
                u = s.back(TURN_LAG)
                if u.batch() and u.t % 2 == 0:
                    wait(dve, turned, u.heads())
                    dve.tensor_copy(probsT[:, u.t % 4, :], ps_turn[0][:, 0:CAUSAL]).then_inc(probsT_even, 1)
                if n.batch():
                    wait(dve, inv_done, n.heads())
                    for b, cols in enumerate(BLOCK_COLS):
                        block_probs = probs[:, n.t % 4, cols]
                        last = dve.tensor_scalar(block_probs, block_probs, inv_total[:, n.t % 4, b:b + 1], None,
                                                 ALU.mult)
                    last.then_inc(norm_done, 1)
                side_work(s)
                if s.number() in LO_AT:
                    lower_weights(LO_AT.index(s.number()))
                if s.number() == LO_AT[1]:
                    dve.wait_ge(small_in, 16 * SMALL_LOADS)
                    dve.wait_ge(consts_ready, CONSTS)

            run(dve, slot_work, DVE_TURN)


def kernel(L0_attn_x, L0_attn_qkv_w, L0_attn_qkv_b, L0_attn_out_w, L0_attn_out_b,
           L0_ffn_W_r, L0_ffn_W_k, L0_ffn_W_v, L0_ffn_mu_r, L0_ffn_mu_k):
    import numpy as np
    from concourse import bacc
    from concourse.bass_utils import run_bass_kernel_spmd

    flat = np.asarray(L0_attn_x).reshape(BATCHES * TOKENS, E)
    by_pair = np.asarray(L0_attn_qkv_b).reshape(PAIRS, 2, 3, D).transpose(1, 3, 2, 0).reshape(P, 3, PAIRS)
    arrays = {
        "x": flat, "xT": flat.T, "qkv_w": L0_attn_qkv_w, "qkv_b": by_pair,
        "out_w": np.asarray(L0_attn_out_w).reshape(HEADS * D, E), "out_b": np.asarray(L0_attn_out_b).reshape(E, 1),
        "w_r": np.asarray(L0_ffn_W_r).T, "w_k": np.asarray(L0_ffn_W_k).T, "w_v": np.asarray(L0_ffn_W_v).T,
        "mu_r": np.asarray(L0_ffn_mu_r).reshape(E, 1), "mu_k": np.asarray(L0_ffn_mu_k).reshape(E, 1),
    }
    arrays = {name: np.ascontiguousarray(a) for name, a in arrays.items()}
    nc = bacc.Bacc("TRN2", target_bir_lowering=False, num_devices=1)
    args = [nc.dram_tensor(name, a.shape, F32, kind="ExternalInput").ap() for name, a in arrays.items()]
    outT = nc.dram_tensor("outT", (E, BATCHES * TOKENS), F32, kind="ExternalOutput").ap()
    build(nc, *args, outT)
    r = run_bass_kernel_spmd(nc, [arrays], core_ids=[0])
    return np.ascontiguousarray(r.results[0]["outT"].T).reshape(BATCHES, TOKENS, E)
```
